# Optimizing a Trainium2 kernel written in Bass

```python
import numpy as np
import jax
import jax.numpy as jnp

def _softmax(x, axis=-1):
    return jax.nn.softmax(x, axis=axis)
def _gelu(x):
    return jax.nn.gelu(x, approximate=True)
def _silu(x):
    return jax.nn.silu(x)
def _sigmoid(x):
    return jax.nn.sigmoid(x)
def _layernorm(x, axis=-1, eps=1e-5):
    m = jnp.mean(x, axis=axis, keepdims=True)
    v = jnp.var(x, axis=axis, keepdims=True)
    return (x - m) / jnp.sqrt(v + eps)
def _scatter_add(tgt, idx, src, axis=0):
    return tgt.at[idx].add(src)
def _segment_sum(src, seg, n):
    return jax.ops.segment_sum(src, seg, n)

kernel_name = 'mk_conv_seq_d2_conv_nhwc96_e85510'

def setup_inputs(seed: int = 0):
    np.random.seed(seed)
    _w = jnp.asarray
    def _rec_inputs():
        import jax
        import jax.numpy as jnp
        _gk = jax.random.key(seed)
        x = -0.000357 + 1 * jax.random.normal(jax.random.fold_in(_gk, 1), (16, 112, 112, 96), jnp.float32)
        return x
    x = _rec_inputs()
    def _L0_conv_setup():
        import jax, jax.numpy as jnp
        import numpy as np
        WS = 7
        SHIFT = 3
        EPS = 0.0001

        def _layer_norm(x, g, b):
            mu = x.mean(-1, keepdims=True)
            var = ((x - mu) ** 2).mean(-1, keepdims=True)
            return (x - mu) / jnp.sqrt(var + EPS) * g + b

        def _relative_position_index(ws):
            coords = np.stack(np.meshgrid(np.arange(ws), np.arange(ws), indexing='ij'))
            cf = coords.reshape(2, -1)
            rel = cf[:, :, None] - cf[:, None, :]
            rel = rel.transpose(1, 2, 0)
            rel[:, :, 0] += ws - 1
            rel[:, :, 1] += ws - 1
            rel[:, :, 0] *= 2 * ws - 1
            return rel.sum(-1)

        def _attn_mask(H, W, ws, shift):
            img = np.zeros((H, W), dtype=np.int32)
            cnt = 0
            for hs in (slice(0, -ws), slice(-ws, -shift), slice(-shift, None)):
                for vs in (slice(0, -ws), slice(-ws, -shift), slice(-shift, None)):
                    img[hs, vs] = cnt
                    cnt += 1
            m = img.reshape(H // ws, ws, W // ws, ws).transpose(0, 2, 1, 3).reshape(-1, ws * ws)
            mask = np.where(m[:, :, None] != m[:, None, :], -100.0, 0.0).astype(np.float32)
            return mask
        key = jax.random.key(seed)
        ks = jax.random.split(key, 8)
        B, H, W, C = (16, 112, 112, 96)
        nH, hidden = (3, 4 * C)
        table = (2 * WS - 1) ** 2
        s = 0.02
        return {'x': jax.random.normal(ks[0], (B, H, W, C), jnp.float32), 'qkv_w': jax.random.normal(ks[1], (C, 3 * C), jnp.float32) * s, 'qkv_b': jnp.zeros((3 * C,), jnp.float32), 'proj_w': jax.random.normal(ks[2], (C, C), jnp.float32) * s, 'proj_b': jnp.zeros((C,), jnp.float32), 'rel_bias': jax.random.normal(ks[3], (table, nH), jnp.float32) * s, 'ln1_g': jnp.ones((C,), jnp.float32), 'ln1_b': jnp.zeros((C,), jnp.float32), 'ln2_g': jnp.ones((C,), jnp.float32), 'ln2_b': jnp.zeros((C,), jnp.float32), 'fc1_w': jax.random.normal(ks[4], (C, hidden), jnp.float32) * s, 'fc1_b': jnp.zeros((hidden,), jnp.float32), 'fc2_w': jax.random.normal(ks[5], (hidden, C), jnp.float32) * s, 'fc2_b': jnp.zeros((C,), jnp.float32)}
    _L0_conv_all = _L0_conv_setup()
    _L0_conv_in = {k: v for k, v in _L0_conv_all.items() if k in ('qkv_w', 'qkv_b', 'proj_w', 'proj_b', 'rel_bias', 'ln1_g', 'ln1_b', 'ln2_g', 'ln2_b', 'fc1_w', 'fc1_b', 'fc2_w', 'fc2_b', )}
    del _L0_conv_all

    def _L1_conv_setup():
        import jax, jax.numpy as jnp
        import numpy as np
        from jax import lax
        BN_EPS = 0.001
        DN = ('NHWC', 'HWIO', 'NHWC')
        key = jax.random.key(seed)
        ks = jax.random.split(key, 8)
        B, H, W, C = (16, 224, 224, 96)
        K = 3
        x = jax.random.normal(ks[0], (B, H, W, C), dtype=jnp.float32)
        dw_kernel = jax.random.normal(ks[1], (K, K, 1, C), dtype=jnp.float32) * 0.1
        dw_bias = jnp.zeros((C,), dtype=jnp.float32)
        pw_kernel = jax.random.normal(ks[2], (1, 1, C, C), dtype=jnp.float32) * 0.1
        pw_bias = jnp.zeros((C,), dtype=jnp.float32)
        gamma = jax.random.uniform(ks[3], (C,), dtype=jnp.float32, minval=0.5, maxval=1.5)
        beta = jax.random.normal(ks[4], (C,), dtype=jnp.float32) * 0.1
        moving_mean = jax.random.normal(ks[5], (C,), dtype=jnp.float32) * 0.1
        moving_var = jax.random.uniform(ks[6], (C,), dtype=jnp.float32, minval=0.5, maxval=1.5)
        return {'x': x, 'dw_kernel': dw_kernel, 'dw_bias': dw_bias, 'pw_kernel': pw_kernel, 'pw_bias': pw_bias, 'gamma': gamma, 'beta': beta, 'moving_mean': moving_mean, 'moving_var': moving_var}
    _L1_conv_all = _L1_conv_setup()
    _L1_conv_in = {k: v for k, v in _L1_conv_all.items() if k in ('dw_kernel', 'dw_bias', 'pw_kernel', 'pw_bias', 'gamma', 'beta', 'moving_mean', 'moving_var', )}
    del _L1_conv_all

    return {
        "x": x,
        "L0_conv_qkv_w": _L0_conv_in["qkv_w"],
        "L0_conv_qkv_b": _L0_conv_in["qkv_b"],
        "L0_conv_proj_w": _L0_conv_in["proj_w"],
        "L0_conv_proj_b": _L0_conv_in["proj_b"],
        "L0_conv_rel_bias": _L0_conv_in["rel_bias"],
        "L0_conv_ln1_g": _L0_conv_in["ln1_g"],
        "L0_conv_ln1_b": _L0_conv_in["ln1_b"],
        "L0_conv_ln2_g": _L0_conv_in["ln2_g"],
        "L0_conv_ln2_b": _L0_conv_in["ln2_b"],
        "L0_conv_fc1_w": _L0_conv_in["fc1_w"],
        "L0_conv_fc1_b": _L0_conv_in["fc1_b"],
        "L0_conv_fc2_w": _L0_conv_in["fc2_w"],
        "L0_conv_fc2_b": _L0_conv_in["fc2_b"],
        "L1_conv_dw_kernel": _L1_conv_in["dw_kernel"],
        "L1_conv_dw_bias": _L1_conv_in["dw_bias"],
        "L1_conv_pw_kernel": _L1_conv_in["pw_kernel"],
        "L1_conv_pw_bias": _L1_conv_in["pw_bias"],
        "L1_conv_gamma": _L1_conv_in["gamma"],
        "L1_conv_beta": _L1_conv_in["beta"],
        "L1_conv_moving_mean": _L1_conv_in["moving_mean"],
        "L1_conv_moving_var": _L1_conv_in["moving_var"],
    }

def reference(x, L0_conv_qkv_w, L0_conv_qkv_b, L0_conv_proj_w, L0_conv_proj_b, L0_conv_rel_bias, L0_conv_ln1_g, L0_conv_ln1_b, L0_conv_ln2_g, L0_conv_ln2_b, L0_conv_fc1_w, L0_conv_fc1_b, L0_conv_fc2_w, L0_conv_fc2_b, L1_conv_dw_kernel, L1_conv_dw_bias, L1_conv_pw_kernel, L1_conv_pw_bias, L1_conv_gamma, L1_conv_beta, L1_conv_moving_mean, L1_conv_moving_var):
    import jax
    import jax.numpy as jnp
    def _L0_conv_ref(x, qkv_w, qkv_b, proj_w, proj_b, rel_bias, ln1_g, ln1_b, ln2_g, ln2_b, fc1_w, fc1_b, fc2_w, fc2_b):
        import jax, jax.numpy as jnp
        import numpy as np
        WS = 7
        SHIFT = 3
        EPS = 0.0001

        def _layer_norm(x, g, b):
            mu = x.mean(-1, keepdims=True)
            var = ((x - mu) ** 2).mean(-1, keepdims=True)
            return (x - mu) / jnp.sqrt(var + EPS) * g + b

        def _relative_position_index(ws):
            coords = np.stack(np.meshgrid(np.arange(ws), np.arange(ws), indexing='ij'))
            cf = coords.reshape(2, -1)
            rel = cf[:, :, None] - cf[:, None, :]
            rel = rel.transpose(1, 2, 0)
            rel[:, :, 0] += ws - 1
            rel[:, :, 1] += ws - 1
            rel[:, :, 0] *= 2 * ws - 1
            return rel.sum(-1)

        def _attn_mask(H, W, ws, shift):
            img = np.zeros((H, W), dtype=np.int32)
            cnt = 0
            for hs in (slice(0, -ws), slice(-ws, -shift), slice(-shift, None)):
                for vs in (slice(0, -ws), slice(-ws, -shift), slice(-shift, None)):
                    img[hs, vs] = cnt
                    cnt += 1
            m = img.reshape(H // ws, ws, W // ws, ws).transpose(0, 2, 1, 3).reshape(-1, ws * ws)
            mask = np.where(m[:, :, None] != m[:, None, :], -100.0, 0.0).astype(np.float32)
            return mask
        B, H, W, C = x.shape
        nH = rel_bias.shape[-1]
        hd = C // nH
        N = WS * WS
        nW = H // WS * (W // WS)
        scale = hd ** (-0.5)
        shortcut = x
        xn = _layer_norm(x, ln1_g, ln1_b)
        xs = jnp.roll(xn, shift=(-SHIFT, -SHIFT), axis=(1, 2))
        wins = xs.reshape(B, H // WS, WS, W // WS, WS, C)
        wins = wins.transpose(0, 1, 3, 2, 4, 5).reshape(-1, N, C)
        qkv = wins @ qkv_w + qkv_b
        qkv = qkv.reshape(-1, N, 3, nH, hd).transpose(2, 0, 3, 1, 4)
        q, k, v = (qkv[0] * scale, qkv[1], qkv[2])
        attn = jnp.einsum('whnd,whmd->whnm', q, k)
        ridx = _relative_position_index(WS)
        bias = rel_bias[jnp.asarray(ridx.reshape(-1))].reshape(N, N, nH).transpose(2, 0, 1)
        attn = attn + bias[None]
        mask = jnp.asarray(_attn_mask(H, W, WS, SHIFT))
        attn = attn.reshape(B, nW, nH, N, N) + mask[None, :, None]
        attn = jax.nn.softmax(attn, axis=-1).reshape(-1, nH, N, N)
        out = jnp.einsum('whnm,whmd->whnd', attn, v)
        out = out.transpose(0, 2, 1, 3).reshape(-1, N, C)
        out = out @ proj_w + proj_b
        out = out.reshape(B, H // WS, W // WS, WS, WS, C)
        out = out.transpose(0, 1, 3, 2, 4, 5).reshape(B, H, W, C)
        out = jnp.roll(out, shift=(SHIFT, SHIFT), axis=(1, 2))
        x = shortcut + out
        y = _layer_norm(x, ln2_g, ln2_b)
        y = jax.nn.gelu(y @ fc1_w + fc1_b)
        y = y @ fc2_w + fc2_b
        return x + y

    def _L1_conv_ref(x, dw_kernel, dw_bias, pw_kernel, pw_bias, gamma, beta, moving_mean, moving_var):
        import jax, jax.numpy as jnp
        import numpy as np
        from jax import lax
        BN_EPS = 0.001
        DN = ('NHWC', 'HWIO', 'NHWC')
        C = x.shape[-1]
        stride = 1
        y = jax.nn.relu(x)
        y = lax.conv_general_dilated(y, dw_kernel, window_strides=(stride, stride), padding='SAME', dimension_numbers=DN, feature_group_count=C)
        y = y + dw_bias
        y = lax.conv_general_dilated(y, pw_kernel, window_strides=(1, 1), padding='SAME', dimension_numbers=DN)
        y = y + pw_bias
        inv = gamma * lax.rsqrt(moving_var + BN_EPS)
        y = y * inv + (beta - moving_mean * inv)
        return y

    def _gn(v, G=32, eps=1e-5):
        B_, H_, W_, C_ = v.shape
        g = v.reshape(B_, H_, W_, G, C_ // G)
        m = jnp.mean(g, axis=(1, 2, 4), keepdims=True)
        s = jnp.var(g, axis=(1, 2, 4), keepdims=True)
        return ((g - m) / jnp.sqrt(s + eps)).reshape(v.shape)

    def _ln_c(v, eps=1e-6):
        m = jnp.mean(v, axis=-1, keepdims=True)
        s = jnp.var(v, axis=-1, keepdims=True)
        return (v - m) / jnp.sqrt(s + eps)

    def _ln_t(v, eps=1e-5):
        m = jnp.mean(v, axis=-1, keepdims=True)
        s = jnp.var(v, axis=-1, keepdims=True)
        return (v - m) / jnp.sqrt(s + eps)

    def _to_tokens(v):
        B_, H_, W_, C_ = v.shape
        return v.reshape(B_, H_ * W_, C_)
    def _from_tokens(t, like):
        return t.reshape(like.shape)

    x = _L0_conv_ref(x, L0_conv_qkv_w, L0_conv_qkv_b, L0_conv_proj_w, L0_conv_proj_b, L0_conv_rel_bias, L0_conv_ln1_g, L0_conv_ln1_b, L0_conv_ln2_g, L0_conv_ln2_b, L0_conv_fc1_w, L0_conv_fc1_b, L0_conv_fc2_w, L0_conv_fc2_b)
    x = _L1_conv_ref(x, L1_conv_dw_kernel, L1_conv_dw_bias, L1_conv_pw_kernel, L1_conv_pw_bias, L1_conv_gamma, L1_conv_beta, L1_conv_moving_mean, L1_conv_moving_var)
    return x


_drawn_inputs = setup_inputs


def setup_inputs(seed=0):
    import zlib

    import numpy as np

    out = dict(_drawn_inputs(seed))
    spreads = {'L0_conv_qkv_b': (0.0, 0.589),
     'L0_conv_proj_b': (0.0, 0.1),
     'L0_conv_ln1_g': (1.0, 0.6),
     'L0_conv_ln1_b': (0.0, 0.8),
     'L0_conv_ln2_g': (1.0, 0.6),
     'L0_conv_ln2_b': (0.0, 2.0),
     'L0_conv_fc1_b': (0.0, 0.483),
     'L0_conv_fc2_b': (0.0, 0.1),
     'L1_conv_dw_bias': (0.0, 0.1),
     'L1_conv_pw_bias': (0.0, 0.1)}
    factors = {'L0_conv_qkv_w': 8.0, 'L0_conv_proj_w': 3.779, 'L0_conv_rel_bias': 8.0}
    for name, (base, spread) in spreads.items():
        noise = np.random.default_rng([zlib.crc32(name.encode()), seed]).standard_normal(out[name].shape)
        drawn = base * np.exp(spread * noise) if base else spread * noise
        out[name] = jnp.asarray(drawn.astype(out[name].dtype))
    for name, factor in factors.items():
        out[name] = (out[name] * factor).astype(out[name].dtype)
    return out
```

```python
from contextlib import ExitStack

import numpy as np

import concourse.bass as bass
from concourse import mybir

ALU = mybir.AluOpType
ACT = mybir.ActivationFunctionType
F32 = mybir.dt.float32
AX_X = mybir.AxisListType.X

WS, SHIFT = 7, 3
NT = WS * WS
HW, C, HEADS = 112, 96, 3
HD = C // HEADS
NWIN = HW // WS
TOK = WS * HW
PT_ = WS * NWIN
HALF = TOK // 2
HID = 4 * C
MC = HID // 128
PAIRS = NWIN // 2
GROUPS = [(0, 3), (3, 3), (6, 2)]
HEAD_ORDER = ((0, 1, 2), (2, 0, 1))
HALVES = ((0, 4), (4, 3))
SCALE = float(HD) ** -0.5
LN_EPS, BN_EPS = 1e-4, 1e-3
MASKED = -100.0

MAP_W = HW + 2
AREA = 10
AREAS = 5
TOP_ROWS, LOW_ROWS = 5, 2

LOOP_FIRST = 6
KEYS = 4 * 16
UNROLL = 4


def swin_conv_kernel(nc, x, qkv_w, qkv_b, proj_w, proj_b, rel_bias_rt, ln1_g, ln1_b, ln2_g, ln2_b,
                     fc1_w, fc1_b, fc2_w, fc2_b, dw_kernel, dw_bias, pw_kernel, pw_bias, gamma, beta,
                     moving_mean, moving_var, eye, rolled_eye, mask, head_blocks, out):
    B = x.shape[0]
    NS = B * NWIN
    LOOPS = (NS - 3 - LOOP_FIRST) // UNROLL

    x_chunks = x.rearrange("b h (c j) f -> (b h c) (j f)", j=WS)
    out_rows = out.rearrange("b h w f -> (b h) w f")

    def nth(strip, tiles, tile):
        if isinstance(strip, int) and strip > NS - 1:
            return tiles * NS
        return tiles * strip + tile + 1

    def wait(eng, sem, count):
        if isinstance(count, int) and count <= 0:
            return
        eng.wait_ge(sem, count)

    def has(strip):
        return not isinstance(strip, int) or 0 <= strip < NS

    def start(value, most):
        if isinstance(value, int):
            return value
        return nc.s_assert_within(value, 0, most,
                                  skip_runtime_bounds_check_because="it follows from the strip's number")

    def steps(eng, step, first=-2):
        for t in range(first, LOOP_FIRST):
            step(t, t % UNROLL)
        with eng.Fori(0, LOOPS) as it:
            for u in range(UNROLL):
                step(it * UNROLL + (LOOP_FIRST + u), (LOOP_FIRST + u) % UNROLL)
        for t in range(LOOP_FIRST + UNROLL * LOOPS, NS + 4):
            step(t, t % UNROLL)

    def is_zero(value, period):
        return 1 - (value + period - 1) // period

    def area_of_strip(s):
        k = s % NWIN
        own = k % 2 + (k + 1) // NWIN + is_zero(s % (2 * NWIN), 2 * NWIN) * 3 \
            + is_zero((s + NWIN) % (2 * NWIN), 2 * NWIN) * 4
        return own * AREA

    def area_below_strip(s):
        k = (s + 1) % NWIN
        below = k % 2 + (k + 1) // NWIN + is_zero((s + 1) % (2 * NWIN), 2 * NWIN) * 4 \
            + is_zero((s + 1 + NWIN) % (2 * NWIN), 2 * NWIN) * 3
        return below * AREA

    with ExitStack() as ctx:
        def sb(name, *shape):
            return ctx.enter_context(nc.sbuf_tensor(name, list(shape), F32))

        def sem(name):
            return ctx.enter_context(nc.semaphore(name))

        ident = sb("ident", 128, 128)
        roll = sb("roll", PT_, PT_)
        heads = sb("heads", 128, 4, C)
        table = sb("table", 128, 2, PAIRS * HEADS, NT)
        wqkv = sb("wqkv", C, 3 * C)
        wproj = sb("wproj", C + 1, C)
        w1 = sb("w1", C, HID)
        w2 = sb("w2", 128, MC, C)
        wpw = sb("wpw", C + 1, C)
        taps = sb("taps", C, 9)
        cols = sb("cols", C, 8)
        bqkv = sb("bqkv", C, 3)
        bfc1 = sb("bfc1", 128, MC)
        minus_half = sb("minus_half", 128, WS)

        x_in = sb("x_in", PT_, 4, WS, C)
        xn = sb("xn", PT_, WS, C)
        x1 = sb("x1", PT_, WS, C)
        x1n = sb("x1n", PT_, WS, C)
        o_tile = sb("o_tile", HW, 2, WS, C)
        xT = sb("xT", C, NWIN, 2, 64)
        qT = sb("qT", C, TOK + 16)
        kT = sb("kT", C, TOK)
        kbd = sb("kbd", C, HEADS + 1, TOK)
        prob = sb("prob", 128, PAIRS * HEADS, 64)
        vbd = sb("vbd", 128, 2, NWIN * C + HD)
        probT = sb("probT", 128, 4, 3, 128)
        attnT = sb("attnT", C + 1, NT, NWIN)
        x1T = sb("x1T", C, TOK)
        hT = sb("hT", 128, MC, TOK)
        acc = sb("acc", C + 1, WS, HW)
        ymap = sb("ymap", C, AREAS * AREA, MAP_W)
        smax = sb("smax", 128, PAIRS * HEADS)
        ssum = sb("ssum", 128, PAIRS * HEADS)
        srec = sb("srec", 128, PAIRS * HEADS)
        ln = [{name: sb(f"{name}{i}", PT_, *shape) for name, shape in
               (("stats", (WS, 6)), ("sum", (WS,)), ("diff", (WS,)), ("dev", (WS,)), ("between", (WS,)),
                ("within", (WS,)), ("minus_mean", (WS,)), ("var_eps", (WS,)), ("rstd", (WS,)),
                ("offset", (WS,)))} for i in (1, 2)]

        bank = [ctx.enter_context(nc.psum_tensor(f"bank{i}", [128, 512], F32)) for i in range(8)]

        const_loaded, rows_loaded = sem("const_loaded"), sem("rows_loaded")
        bias_loaded, bias_doubled, row_moved = sem("bias_loaded"), sem("bias_doubled"), sem("row_moved")
        pool_cleared, dve_set, pe_set, pool_set = sem("pool_cleared"), sem("dve_set"), sem("pe_set"), sem("pool_set")
        x_loaded = [sem(f"x_loaded{i}") for i in range(4)]
        out_stored = [sem(f"out_stored{i}") for i in range(2)]
        k_ready = sem("k_ready")
        xt_psum, q_psum, k_psum, v_psum = sem("xt_psum"), sem("q_psum"), sem("k_psum"), sem("v_psum")
        s_psum, pt_psum, o_psum, proj_psum = sem("s_psum"), sem("pt_psum"), sem("o_psum"), sem("proj_psum")
        x1t_psum, h_psum, y_psum, yt_psum = sem("x1t_psum"), sem("h_psum"), sem("y_psum"), sem("yt_psum")
        pw_psum = sem("pw_psum")
        xt_ready, q_ready, k_copied, exp_done = sem("xt_ready"), sem("q_ready"), sem("k_copied"), sem("exp_done")
        pt_ready, o_ready, x1t_ready = sem("pt_ready"), sem("o_ready"), sem("x1t_ready")
        h_ready, ymap_ready, out_ready = sem("h_ready"), sem("ymap_ready"), sem("out_ready")
        xn_ready, x1n_ready = sem("xn_ready"), sem("x1n_ready")
        s_biased, max_ready, sum_done, rec_ready = sem("s_biased"), sem("max_ready"), sem("sum_done"), sem("rec_ready")
        v_ready, y_ready, x1_ready = sem("v_ready"), sem("y_ready"), sem("x1_ready")
        stats_done = [sem("stats1_done"), sem("stats2_done")]
        parts_done = [sem("parts1_done"), sem("parts2_done")]
        halves_done = [sem("halves1_done"), sem("halves2_done")]
        ln_ready = [sem("ln1_ready"), sem("ln2_ready")]
        top_done, low_done = sem("top_done"), sem("low_done")
        shifted, p_ready = sem("shifted"), sem("p_ready")
        rstd_done = [sem("rstd1_done"), sem("rstd2_done")]
        scale_ready = [sem("scale1_ready"), sem("scale2_ready")]

        bias0 = hT[:, 0, 0:HEADS * NT]
        maskt = hT[:, 1, 0:4 * NT].rearrange("p (a b m) -> p a b m", a=2, b=2)
        pw_raw = hT[0:C, 2, 0:C]
        qkv_raw = hT[0:C, 2, C:4 * C]
        proj_row = hT[0:1, 2, 4 * C:5 * C]
        w1_raw = x1T[:, 0:HID]
        rows = x1[0:1].rearrange("p j f -> p (j f)")
        proj_b_row, pw_b_row, gamma_row, beta_row, mean_row, var_row, one_row = (
            rows[:, i * C:(i + 1) * C] for i in range(7))
        scratch = x1n[0:1].rearrange("p j f -> p (j f)")
        inv_row, var_eps, row_a, row_b, pw_row, std_row, mh_row = (scratch[:, i * C:(i + 1) * C] for i in range(7))

        block = ctx.enter_context(nc.Block())

        @block.sync
        def _(sp):
            const = [
                (ident[:], eye), (roll[:], rolled_eye), (heads[:], head_blocks), (maskt, mask),
                (qkv_raw, qkv_w), (wproj[0:C], proj_w), (w1_raw, fc1_w),
                (w2[:], fc2_w.rearrange("(m p) n -> p m n", p=128)),
                (pw_raw, pw_kernel.rearrange("a b i o -> (a b i) o")),
                (taps[:], dw_kernel),
                (bqkv[:], qkv_b),
                (bfc1[:], fc1_b),
            ] + [(cols[:, i:i + 1], v.rearrange("(f u) -> f u", u=1))
                 for i, v in enumerate((ln1_g, ln1_b, ln2_g, ln2_b, fc2_b, dw_bias))]
            for dst, src in const:
                sp.dma_start(dst, src).then_inc(const_loaded, 16)
            for dst, src in ((proj_b_row, proj_b), (pw_b_row, pw_bias), (gamma_row, gamma), (beta_row, beta),
                             (mean_row, moving_mean), (var_row, moving_var)):
                sp.dma_start(dst, src.rearrange("(u f) -> u f", u=1)).then_inc(rows_loaded, 16)

            def load(t, phase):
                s = t + 3
                if not has(s):
                    return
                slot = (phase + 3) % UNROLL
                wait(sp, x1_ready, nth(t - 1, 2, 1))
                image, k = s // NWIN, s % NWIN
                first = (image * HW + k * WS + SHIFT) * NWIN
                wrapped = (image * HW + (k + 1) % NWIN * WS) * NWIN
                top = (WS - SHIFT) * NWIN
                dst = x_in[:, slot].rearrange("p j f -> p (j f)")
                sp.dma_start(dst[0:top], x_chunks[bass.ds(start(first, B * HW * NWIN - top), top)]).then_inc(x_loaded[slot], 16)
                sp.dma_start(dst[top:PT_], x_chunks[bass.ds(start(wrapped, B * HW * NWIN - (PT_ - top)), PT_ - top)]).then_inc(x_loaded[slot], 16)

            def spread_keys(t):
                if not has(t + 1):
                    return
                wait(sp, s_psum, nth(t, 3, 2))
                wait(sp, k_copied, nth(t + 1, 2, 1))
                for h, part in ((0, 1), (1, 2), (2, 0), (2, 3)):
                    hp = slice(h * HD, (h + 1) * HD)
                    sp.dma_start(kbd[hp, part, :], kT[hp, :]).then_inc(k_ready, 16)

            def store(t, phase):
                i = t - 4
                if not has(i):
                    return
                slot = phase % 2
                wait(sp, out_ready, nth(i, 2, 1))
                image, k = i // NWIN, (i + 1) % NWIN
                top = image * HW + k * WS + 2
                low = image * HW + (k + 1) % NWIN * WS
                for row, at, n in ((top, 0, TOP_ROWS), (low, TOP_ROWS, LOW_ROWS)):
                    sp.dma_start(out_rows[bass.ds(start(row, B * HW - n), n)].rearrange("r w f -> w r f"),
                                 o_tile[:, slot, at:at + n]).then_inc(out_stored[slot], 16)

            def step(t, phase):
                load(t, phase)
                spread_keys(t)
                store(t, phase)

            sp.wait_ge(pool_cleared, 1)
            side = 2 * WS - 1
            for jx in range(WS):
                for ry in range(WS):
                    n = jx * WS + ry
                    src = rel_bias_rt[:, WS - 1 - jx:side - jx, WS - 1 - ry:side - ry]
                    sp.dma_start(bias0[n:n + 1], src).then_inc(bias_loaded, 16)
            load(-3, 1)
            sp.wait_ge(bias_loaded, 16 * NT)
            sp.dma_start(bias0[64:64 + NT], bias0[0:NT]).then_inc(bias_doubled, 16)
            sp.wait_ge(dve_set, 6)
            sp.dma_start(wproj[C:C + 1], proj_row).then_inc(row_moved, 16)
            sp.wait_ge(dve_set, 12)
            sp.dma_start(wpw[C:C + 1], pw_row).then_inc(row_moved, 16)

            sp.wait_ge(pool_cleared, 2)
            steps(sp, step)
            stores = [(NS + 1) // 2, NS // 2]
            sp.wait_ge(out_stored[1], 32 * stores[0])
            sp.wait_ge(out_stored[0], 32 * stores[1])

        @block.tensor
        def _(pe):
            pe.wait_ge(const_loaded, 16 * 18)
            pe.wait_ge(rows_loaded, 16 * 6)
            for i in range(3):
                pe.matmul(bank[0][0:C, i:i + 1], qkv_raw[:, i * C:(i + 1) * C], cols[:, 1:2], start=True, stop=True)
            for m in range(MC):
                pe.matmul(bank[1][:, m:m + 1], w1_raw[:, m * 128:(m + 1) * 128], cols[:, 3:4], start=True, stop=True)
            pe.matmul(bank[2][0:1, 0:C], cols[:, 5:6], pw_raw, start=True, stop=True).then_inc(pe_set, 1)
            pe.wait_ge(dve_set, 3)
            pe.matmul(bank[3][0:1, 0:C], bqkv[:, 2:3], wproj[0:C], start=True, stop=True).then_inc(pe_set, 1)
            pe.wait_ge(dve_set, 9)
            pe.matmul(bank[4][0:C, 0:C], one_row, inv_row, start=True, stop=True).then_inc(pe_set, 1)
            pe.wait_ge(dve_set, 14)
            pe.wait_ge(row_moved, 32)
            pe.wait_ge(pool_cleared, 2)

            def scores(t):
                if not has(t):
                    return
                wait(pe, q_ready, nth(t, 2, 1))
                wait(pe, k_ready, KEYS * nth(t, 1, 0))
                for g, (first, n) in enumerate(GROUPS):
                    if g == 0:
                        wait(pe, xt_ready, nth(t + 1, 2, 1))
                    elif g == 1:
                        wait(pe, y_ready, nth(t - 2, 2, 1))
                    else:
                        wait(pe, ymap_ready, nth(t - 2, 2, 1))
                    for p in range(n):
                        for side in range(2):
                            w = 2 * (first + p) + side
                            mm = pe.matmul(bank[g][64 * side:64 * side + 64, p * HEADS * NT:(p + 1) * HEADS * NT],
                                           qT[:, w * NT:w * NT + 64],
                                           kbd[:, 1 - (first + p) % 2:4 - (first + p) % 2, w * NT:(w + 1) * NT],
                                           start=True, stop=True)
                    mm.then_inc(s_psum, 1)

            def queries_keys(t):
                if not has(t + 1):
                    return
                wait(pe, xt_ready, nth(t + 1, 2, 1))
                for u in range(2):
                    if u == 0:
                        wait(pe, pt_ready, nth(t - 1, 4, 1))
                    else:
                        wait(pe, ymap_ready, nth(t - 2, 2, 0))
                    pe.matmul(bank[3 + u][0:C, 0:HALF], wqkv[:, 0:C], xT[:, 8 * u:8 * u + 8, 0, 0:NT],
                              start=True, stop=True).then_inc(q_psum, 1)
                for u in range(2):
                    if u == 0:
                        wait(pe, x1_ready, nth(t - 1, 2, 0))
                    else:
                        wait(pe, o_ready, nth(t - 1, 2, 1))
                    pe.matmul(bank[5 + u][0:C, 0:HALF], wqkv[:, C:2 * C], xT[:, 8 * u:8 * u + 8, 0, 0:NT],
                              start=True, stop=True).then_inc(k_psum, 1)

            def values(t):
                if not has(t + 1):
                    return
                for i in range(4):
                    if i < 2:
                        wait(pe, s_biased, nth(t, 3, i + 1))
                    else:
                        wait(pe, q_ready, nth(t + 1, 2, i - 2))
                    for j in range(4):
                        w = 4 * i + j
                        mm = pe.matmul(bank[1 + i][:, j * C:(j + 1) * C], xT[:, w], wqkv[:, 2 * C:3 * C],
                                       start=True, stop=True)
                    mm.then_inc(v_psum, 1)

            def turn_x1(t):
                if not has(t - 1):
                    return
                wait(pe, x1n_ready, nth(t - 1, 1, 0))
                for i, (js, b) in enumerate(((range(0, 4), 7), (range(4, 7), 0))):
                    if i == 0:
                        wait(pe, x1_ready, nth(t - 1, 2, 1))
                        wait(pe, out_ready, nth(t - 4, 2, 0))
                    else:
                        wait(pe, s_biased, nth(t, 3, 0))
                        wait(pe, out_ready, nth(t - 4, 2, 1))
                    for a, j in enumerate(js):
                        mm = pe.transpose(bank[b][0:C, a * PT_:(a + 1) * PT_], x1n[:, j, :], ident[0:PT_, 0:PT_])
                    mm.then_inc(x1t_psum, 1)

            def mlp(t):
                if not has(t - 1):
                    return
                for i in range(2 * MC):
                    half, m = i // MC, i % MC
                    first, n = ((0, 4), (4, 3))[half]
                    if m == 0:
                        wait(pe, x1t_ready, nth(t - 1, 2, half))
                    if i < 2:
                        wait(pe, k_copied, nth(t + 1, 2, i))
                    elif i == 2:
                        wait(pe, x1t_ready, nth(t - 1, 2, 0))
                    else:
                        wait(pe, h_ready, nth(t - 1, 6, i - 3))
                    pe.matmul(bank[5 + i % 3][:, 0:n * PT_], w1[:, m * 128:(m + 1) * 128],
                              x1T[:, first * PT_:(first + n) * PT_], start=True, stop=True).then_inc(h_psum, 1)
                for half, (first, n) in enumerate(((0, 4), (4, 3))):
                    wait(pe, h_ready, nth(t - 1, 6, 3 * half + 2))
                    if half == 0:
                        wait(pe, x1t_ready, nth(t - 1, 2, 1))
                    else:
                        wait(pe, v_ready, nth(t + 1, 4, 0))
                    for a in range(n):
                        j = first + a
                        for m in range(MC):
                            mm = pe.matmul(bank[half][0:PT_, a * C:(a + 1) * C], hT[:, m, j * PT_:(j + 1) * PT_],
                                           w2[:, m, :], start=(m == 0), stop=(m == MC - 1))
                    mm.then_inc(y_psum, 1)

            def turn_probs(t, d):
                wait(pe, p_ready, nth(t, 3, (2 * d + 1) // 3))
                if d < 3:
                    wait(pe, v_ready, nth(t + 1, 4, d + 1))
                else:
                    wait(pe, pt_ready, nth(t, 4, 0))
                b = bank[(2, 3, 4, 2)[d]]
                for i, slot in enumerate((0, 4, 2)):
                    mm = pe.transpose(b[:, i * 128:(i + 1) * 128], prob[:, 6 * d + slot:6 * d + slot + 2, :], ident[:])
                mm.then_inc(pt_psum, 1)

            def weigh_values(t, phase, d):
                if d == 0:
                    wait(pe, v_ready, nth(t, 4, 3))
                    wait(pe, h_ready, nth(t - 1, 6, 3))
                if d == 2:
                    wait(pe, h_ready, nth(t - 1, 6, 4))
                wait(pe, pt_ready, nth(t, 4, d))
                b, v = bank[5 + d // 2], vbd[:, phase % 2]
                for j in range(4):
                    w = 4 * d + j
                    at = (w % 8) * NT
                    side = 64 * (j % 2)
                    pe.matmul(b[0:64, at:at + NT], v[:, w * C:w * C + 64],
                              probT[:, d, j // 2, side:side + NT], start=True, stop=True)
                    mm = pe.matmul(b[64:128, at:at + NT], v[:, w * C + 64:w * C + 128],
                                   probT[:, d, 2, side:side + NT], start=True, stop=True)
                if d % 2:
                    mm.then_inc(o_psum, 1)

            def attend(t, phase):
                if not has(t):
                    return
                turn_probs(t, 0)
                turn_probs(t, 1)
                turn_probs(t, 2)
                weigh_values(t, phase, 0)
                turn_probs(t, 3)
                for d in range(1, 4):
                    weigh_values(t, phase, d)

            def turn_x(t):
                if not has(t + 2):
                    return
                wait(pe, xn_ready, nth(t + 2, 1, 0))
                for i, (js, perm, b) in enumerate(((range(3, 7), ident[0:PT_, 0:PT_], 7),
                                                   (range(0, 3), roll[:], 0))):
                    if i == 0:
                        wait(pe, h_ready, nth(t - 1, 6, 5))
                    else:
                        wait(pe, y_ready, nth(t - 1, 2, 0))
                    for a, j in enumerate(js):
                        mm = pe.transpose(bank[b][0:C, a * PT_:(a + 1) * PT_], xn[:, j, :], perm)
                    mm.then_inc(xt_psum, 1)

            def pointwise(t):
                if not has(t - 4):
                    return
                wait(pe, top_done, nth(t - 4, 9, 8))
                wait(pe, low_done, nth(t - 4, 9, 8))
                for i, ((first, n), b) in enumerate(zip(HALVES, (7, 0))):
                    if i == 0:
                        wait(pe, x1_ready, nth(t - 1, 2, 1))
                    else:
                        wait(pe, s_biased, nth(t, 3, 0))
                    wait(pe, out_ready, nth(t - 5, 2, i))
                    for a in range(n):
                        mm = pe.matmul(bank[b][0:HW, a * C:(a + 1) * C], acc[:, first + a, :], wpw[:],
                                       start=True, stop=True)
                    mm.then_inc(pw_psum, 1)

            def turn_y(t):
                if not has(t - 1):
                    return
                for i, (first, n, b) in enumerate(((0, 4, 4), (4, 3, 2))):
                    wait(pe, y_ready, nth(t - 1, 2, i))
                    wait(pe, pt_ready, nth(t, 4, i + 2))
                    for a in range(n):
                        mm = pe.transpose(bank[b][0:C, a * PT_:(a + 1) * PT_], x1[:, first + a, :],
                                          ident[0:PT_, 0:PT_])
                    mm.then_inc(yt_psum, 1)

            def project(t):
                if not has(t):
                    return
                wait(pe, o_ready, nth(t, 2, 1))
                for i, (first, n, b) in enumerate(((0, 4, 5), (4, 3, 7))):
                    if i == 1:
                        wait(pe, xt_ready, nth(t + 2, 2, 0))
                    for a in range(n):
                        j = first + a
                        col = j - SHIFT if j >= SHIFT else j - SHIFT + WS
                        mm = pe.matmul(bank[b][0:PT_, a * C:(a + 1) * C],
                                       attnT[:, col * WS:(col + 1) * WS, :], wproj[:],
                                       start=True, stop=True)
                    mm.then_inc(proj_psum, 1)

            def step(t, phase):
                scores(t)
                queries_keys(t)
                pointwise(t)
                values(t)
                turn_x1(t)
                mlp(t)
                attend(t, phase)
                turn_x(t)
                turn_y(t)
                project(t)

            steps(pe, step)

        @block.scalar
        def _(act):
            act.wait_ge(dve_set, 14)
            act.wait_ge(pool_cleared, 2)

            def exps(t, g):
                if not has(t):
                    return
                first, n = GROUPS[g]
                wait(act, shifted, nth(t, 3, g))
                p = prob[:, HEADS * first:HEADS * (first + n), 0:NT]
                act.activation(p, p, ACT.Exp).then_inc(exp_done, 1)

            def queries_keys(t):
                if not has(t + 1):
                    return
                wait(act, s_psum, nth(t, 3, 2))
                for u in range(2):
                    wait(act, q_psum, nth(t + 1, 2, u))
                    act.activation(qT[:, u * HALF:(u + 1) * HALF], bank[3 + u][0:C, 0:HALF], ACT.Identity,
                                   bias=bqkv[:, 0:1], scale=SCALE).then_inc(q_ready, 1)
                wait(act, k_ready, KEYS * nth(t, 1, 0))
                for u in range(2):
                    wait(act, k_psum, nth(t + 1, 2, u))
                    act.activation(kT[:, u * HALF:(u + 1) * HALF], bank[5 + u][0:C, 0:HALF], ACT.Identity,
                                   bias=bqkv[:, 1:2]).then_inc(k_copied, 1)

            def outputs(t, phase):
                if not has(t - 4):
                    return
                slot = phase % 2
                wait(act, out_stored[slot], 32 * ((t - 4) // 2))
                for i, ((first, n), b) in enumerate(zip(HALVES, (7, 0))):
                    wait(act, pw_psum, nth(t - 4, 2, i))
                    act.copy(o_tile[:, slot, first:first + n],
                             bank[b][0:HW, 0:n * C].rearrange("p (r f) -> p r f", r=n)).then_inc(out_ready, 1)

            def normalise(which, s, dst, src, ready):
                b = ln[which]
                wait(act, scale_ready[which], nth(s, 1, 0))
                for j in range(WS):
                    last = act.activation(dst[:, j], src[:, j], ACT.Identity, bias=b["offset"][:, j:j + 1],
                                          scale=b["rstd"][:, j:j + 1])
                last.then_inc(ready, 1)

            def x1_turned(t):
                if not has(t - 1):
                    return
                wait(act, h_psum, nth(t - 2, 6, 5))
                for i, (first, n, b) in enumerate(((0, 4, 7), (4, 3, 0))):
                    wait(act, x1t_psum, nth(t - 1, 2, i))
                    act.copy(x1T[:, first * PT_:(first + n) * PT_], bank[b][0:C, 0:n * PT_]).then_inc(x1t_ready, 1)

            def gelus(t):
                if not has(t - 1):
                    return
                wait(act, y_psum, nth(t - 2, 2, 1))
                for i in range(2 * MC):
                    half, m = i // MC, i % MC
                    first, n = ((0, 4), (4, 3))[half]
                    wait(act, h_psum, nth(t - 1, 6, i))
                    act.activation(hT[:, m, first * PT_:(first + n) * PT_], bank[5 + i % 3][:, 0:n * PT_],
                                   ACT.Gelu_apprx_tanh, bias=bfc1[:, m:m + 1]).then_inc(h_ready, 1)

            def probs_turned(t):
                if not has(t):
                    return
                wait(act, o_psum, nth(t - 1, 2, 1))
                for d in range(4):
                    wait(act, pt_psum, nth(t, 4, d))
                    act.copy(probT[:, d].rearrange("p i n -> p (i n)"), bank[(2, 3, 4, 2)[d]][:, 0:384])\
                        .then_inc(pt_ready, 1)

            def attention_out(t):
                if not has(t):
                    return
                wait(act, proj_psum, nth(t - 1, 2, 1))
                far = (WS - SHIFT) * WS
                for u in range(2):
                    wait(act, o_psum, nth(t, 2, u))
                    src = bank[5 + u][0:C, 0:8 * NT].rearrange("p (w n) -> p w n", w=8)
                    dst = attnT[0:C].rearrange("p n w -> p w n")
                    act.copy(dst[:, 8 * u:8 * u + 8, 0:far], src[:, :, 0:far])
                    inner = 8 - u
                    last = act.copy(dst[:, 8 * u + 1:8 * u + 1 + inner, far:], src[:, 0:inner, far:])
                    if u == 1:
                        last = act.copy(dst[:, 0, far:], src[:, 7, far:])
                    last.then_inc(o_ready, 1)

            def x_turned(t):
                if not has(t + 2):
                    return
                wait(act, v_psum, nth(t + 1, 4, 3))
                for i, (first, n, b) in enumerate(((0, 4, 7), (4, 3, 0))):
                    wait(act, xt_psum, nth(t + 2, 2, i))
                    src = bank[b][0:C, 0:n * PT_].rearrange("p (n w) -> p n w", w=NWIN)
                    src = src.unsqueeze(1).broadcast_to([C, 2, n * WS, NWIN])
                    dst = xT[:].rearrange("p w d n -> p d n w")[:, :, first * WS:(first + n) * WS, :]
                    act.copy(dst, src).then_inc(xt_ready, 1)

            def into_map(t, phase):
                if not has(t - 1):
                    return
                s = t - 1
                wait(act, top_done, nth(t - 3, 9, 8))
                wait(act, low_done, nth(t - 3, 9, 8))
                area = area_of_strip(s)
                if phase == 0:
                    parts = [(0, 4, area + 2), (4, 3, area + 6 + (s % NWIN + 1) // NWIN)]
                else:
                    parts = [(0, 7, area + 2)]
                parts.append((5, 2, area_below_strip(s)))
                for i, ((first, n), b) in enumerate(zip(HALVES, (4, 2))):
                    wait(act, yt_psum, nth(s, 2, i))
                    src = bank[b][0:C, 0:n * PT_].rearrange("p (j r c) -> p j r c", j=n, r=WS)
                    for r0, nr, row in parts:
                        dst = ymap[:, bass.ds(start(row, AREAS * AREA - nr), nr), 1:1 + HW].rearrange("p r (c j) -> p j r c", j=WS)
                        last = act.activation(dst[:, first:first + n], src[:, :, r0:r0 + nr, :], ACT.Relu,
                                              bias=cols[:, 4:5])
                    last.then_inc(ymap_ready, 1)

            def step(t, phase):
                queries_keys(t)
                outputs(t, phase)
                if has(t - 1):
                    wait(act, x1t_psum, nth(t - 2, 2, 1))
                    normalise(1, t - 1, x1n, x1, x1n_ready)
                exps(t, 0)
                exps(t, 1)
                x1_turned(t)
                exps(t, 2)
                gelus(t)
                if has(t + 2):
                    wait(act, xt_psum, nth(t + 1, 2, 1))
                    normalise(0, t + 2, xn, x_in[:, (phase + 2) % UNROLL], xn_ready)
                probs_turned(t)
                attention_out(t)
                x_turned(t)
                into_map(t, phase)

            steps(act, step)

        @block.vector
        def _(dve):
            dve.memset(attnT[C:C + 1], 1.0)
            dve.memset(acc[C:C + 1], 1.0)
            dve.memset(one_row, 1.0).then_inc(dve_set, 1)
            dve.wait_ge(const_loaded, 16 * 18)
            dve.wait_ge(rows_loaded, 16 * 6)
            dve.wait_ge(pe_set, 1)
            dve.tensor_tensor(bfc1[:], bank[1][:, 0:MC], bfc1[:], ALU.add).then_inc(dve_set, 1)
            dve.tensor_tensor(bqkv[:], bank[0][0:C, 0:3], bqkv[:], ALU.add).then_inc(dve_set, 1)
            dve.wait_ge(dve_set, 3)
            dve.tensor_scalar(bqkv[:, 0:1], bqkv[:, 0:1], SCALE, None, ALU.mult).then_inc(dve_set, 1)
            dve.tensor_scalar(wqkv[:], qkv_raw, cols[:, 0:1], None, ALU.mult).then_inc(dve_set, 1)
            dve.wait_ge(pe_set, 2)
            dve.tensor_tensor(proj_row, bank[3][0:1, 0:C], proj_b_row, ALU.add).then_inc(dve_set, 1)
            dve.tensor_scalar(w1[:], w1_raw, cols[:, 2:3], None, ALU.mult).then_inc(dve_set, 1)
            dve.tensor_scalar(var_eps, var_row, BN_EPS, None, ALU.add).then_inc(dve_set, 1)
            dve.wait_ge(pool_set, 1)
            dve.tensor_tensor(inv_row, std_row, gamma_row, ALU.mult).then_inc(dve_set, 1)
            dve.tensor_tensor(row_a, bank[2][0:1, 0:C], pw_b_row, ALU.add).then_inc(dve_set, 1)
            dve.wait_ge(dve_set, 10)
            dve.tensor_tensor(row_b, row_a, mean_row, ALU.subtract).then_inc(dve_set, 1)
            dve.wait_ge(dve_set, 11)
            dve.tensor_tensor(row_a, row_b, inv_row, ALU.mult).then_inc(row_step := sem("row_step"), 1)
            dve.wait_ge(row_step, 1)
            dve.tensor_tensor(pw_row, row_a, beta_row, ALU.add).then_inc(dve_set, 1)
            dve.wait_ge(pe_set, 3)
            dve.tensor_tensor(wpw[0:C], bank[4][0:C, 0:C], pw_raw, ALU.mult).then_inc(dve_set, 1)
            dve.wait_ge(bias_doubled, 16)
            for last_strip in range(2):
                for p in range(PAIRS):
                    m = maskt[:, last_strip, p // (PAIRS - 1)]
                    for i, h in enumerate(HEAD_ORDER[p % 2]):
                        last = dve.tensor_tensor(table[:, last_strip, HEADS * p + i], bias0[:, h * NT:(h + 1) * NT],
                                                 m, ALU.add)
            last.then_inc(dve_set, 1)
            dve.wait_ge(dve_set, 14)
            dve.wait_ge(pool_cleared, 2)
            dve.wait_ge(row_moved, 32)

            def add_bias(t, phase, g):
                if not has(t):
                    return
                first, n = GROUPS[g]
                if g == 0:
                    wait(dve, pt_psum, nth(t - 1, 4, 3))
                wait(dve, s_psum, nth(t, 3, g))
                which = (t % NWIN + 1) // NWIN if phase == UNROLL - 1 else 0
                bias = (table[:, which] if isinstance(which, int) else table[:, bass.ds(start(which, 1), 1)].squeeze(1))
                dst = prob[:, HEADS * first:HEADS * (first + n), 0:NT]
                dve.tensor_tensor(dst,
                                  bank[g][:, 0:n * HEADS * NT].rearrange("p (a m) -> p a m", m=NT),
                                  bias[:, HEADS * first:HEADS * (first + n)],
                                  ALU.add).then_inc(s_biased, 1)

            def find_max(t, g):
                if not has(t):
                    return
                first, n = GROUPS[g]
                at = slice(HEADS * first, HEADS * (first + n))
                wait(dve, s_biased, nth(t, 3, g))
                dve.tensor_reduce(smax[:, at], prob[:, at, 0:NT], AX_X, ALU.max).then_inc(max_ready, 1)

            def add_up(t, g):
                if not has(t):
                    return
                first, n = GROUPS[g]
                at = slice(HEADS * first, HEADS * (first + n))
                wait(dve, exp_done, nth(t, 3, g))
                p = prob[:, HEADS * first:HEADS * (first + n), 0:NT]
                dve.tensor_reduce(ssum[:, at], p, AX_X, ALU.add).then_inc(sum_done, 1)
                wait(dve, sum_done, nth(t, 3, g))
                dve.reciprocal(srec[:, at], ssum[:, at]).then_inc(rec_ready, 1)

            def tap(t, i):
                c = t - 3
                if not has(c):
                    return
                dy, dx = i // 3 - 1, i % 3
                top = area_below_strip(c) + 1 + dy
                low = top + TOP_ROWS + ((c + 1) % NWIN + 1) // NWIN
                if i == 0:
                    wait(dve, ymap_ready, nth(c + 1, 2, 1))
                    wait(dve, pw_psum, nth(t - 4, 2, 1))
                for row, at, n, done in ((top, 0, TOP_ROWS, top_done), (low, TOP_ROWS, LOW_ROWS, low_done)):
                    src = ymap[:, bass.ds(start(row, AREAS * AREA - n), n), dx:dx + HW]
                    dst = acc[0:C, at:at + n, :]
                    if i == 0:
                        dve.tensor_scalar(dst, src, taps[:, 0:1], None, ALU.mult).then_inc(done, 1)
                    else:
                        wait(dve, done, nth(c, 9, i - 1))
                        dve.scalar_tensor_tensor(out=dst, in0=src, scalar=taps[:, i:i + 1], in1=dst,
                                                 op0=ALU.mult, op1=ALU.add).then_inc(done, 1)

            def values(t, phase, i):
                if not has(t + 1):
                    return
                wait(dve, o_psum, nth(t - 1, 2, 1))
                wait(dve, v_psum, nth(t + 1, 4, i))
                dst = vbd[:, (phase + 1) % 2, 4 * i * C:4 * (i + 1) * C].rearrange("p (w f) -> p w f", w=4)
                dve.tensor_tensor(dst, bank[1 + i][:, 0:4 * C].rearrange("p (w f) -> p w f", w=4), heads[:],
                                  ALU.mult).then_inc(v_ready, 1)

            def norm_stats(which, s, src, eps):
                b = ln[which]
                for j in range(WS):
                    last = dve.bn_stats(b["stats"][:, j], src[:, j])
                last.then_inc(stats_done[which], 1)
                st = b["stats"]
                wait(dve, stats_done[which], nth(s, 1, 0))
                dve.tensor_tensor(b["sum"][:], st[:, :, 1], st[:, :, 4], ALU.add)
                dve.tensor_tensor(b["diff"][:], st[:, :, 1], st[:, :, 4], ALU.subtract)
                dve.tensor_tensor(b["dev"][:], st[:, :, 2], st[:, :, 5], ALU.add).then_inc(parts_done[which], 1)
                wait(dve, parts_done[which], nth(s, 1, 0))
                dve.tensor_scalar(b["minus_mean"][:], b["sum"][:], -0.5, None, ALU.mult)
                dve.scalar_tensor_tensor(out=b["between"][:], in0=b["diff"][:], scalar=0.25, in1=b["diff"][:],
                                         op0=ALU.mult, op1=ALU.mult)
                dve.tensor_scalar(b["within"][:], b["dev"][:], 1.0 / C, eps, ALU.mult, ALU.add)\
                    .then_inc(halves_done[which], 1)
                wait(dve, halves_done[which], nth(s, 1, 0))
                dve.tensor_tensor(b["var_eps"][:], b["between"][:], b["within"][:], ALU.add)\
                    .then_inc(ln_ready[which], 1)

            def norm_x(t, phase):
                if not has(t + 2):
                    return
                slot = (phase + 2) % UNROLL
                wait(dve, xn_ready, nth(t + 1, 1, 0))
                wait(dve, x_loaded[slot], 32 * ((t + 2) // UNROLL + 1))
                norm_stats(0, t + 2, x_in[:, slot], LN_EPS)

            def add_x1(t):
                if not has(t - 1):
                    return
                wait(dve, x1n_ready, nth(t - 1, 1, 0))
                wait(dve, x1_ready, nth(t - 1, 2, 1))
                for i, (first, n) in enumerate(((0, 4), (4, 3))):
                    wait(dve, y_psum, nth(t - 1, 2, i))
                    js = slice(first, first + n)
                    dve.tensor_tensor(x1[:, js], bank[i][0:PT_, 0:n * C].rearrange("p (j f) -> p j f", j=n),
                                      x1[:, js], ALU.add).then_inc(y_ready, 1)

            def add_x(t, phase):
                if not has(t):
                    return
                wait(dve, yt_psum, nth(t - 1, 2, 1))
                for i, (first, n, b) in enumerate(((0, 4, 5), (4, 3, 7))):
                    wait(dve, proj_psum, nth(t, 2, i))
                    js = slice(first, first + n)
                    dve.tensor_tensor(x1[:, js], bank[b][0:PT_, 0:n * C].rearrange("p (j f) -> p j f", j=n),
                                      x_in[:, phase, js], ALU.add).then_inc(x1_ready, 1)
                wait(dve, x1_ready, nth(t, 2, 1))
                norm_stats(1, t, x1, LN_EPS)

            def step(t, phase):
                for g in range(3):
                    add_bias(t, phase, g)
                for g in range(3):
                    find_max(t, g)
                tap(t, 0)
                tap(t, 1)
                values(t, phase, 0)
                values(t, phase, 1)
                add_up(t, 0)
                add_up(t, 1)
                values(t, phase, 2)
                values(t, phase, 3)
                add_up(t, 2)
                norm_x(t, phase)
                tap(t, 2)
                tap(t, 3)
                add_x1(t)
                for i in range(4, 9):
                    tap(t, i)
                add_x(t, phase)

            steps(dve, step)

        @block.gpsimd
        def _(pool):
            pool.memset(bias0, 0.0).then_inc(pool_cleared, 1)
            pool.memset(mh_row, -0.5)
            pool.memset(minus_half[:], -0.5)
            pool.memset(kbd[:], 0.0)
            pool.memset(prob[:], 0.0)
            pool.memset(vbd[:, :, NWIN * C:], 0.0)
            pool.memset(xT[:], 0.0)
            pool.memset(qT[:, TOK:], 0.0)
            pool.memset(ymap[:], 0.0).then_inc(pool_cleared, 1)
            pool.wait_ge(pool_cleared, 2)
            pool.wait_ge(dve_set, 8)
            pool.tensor_tensor(std_row, var_eps, mh_row, ALU.pow).then_inc(pool_set, 1)

            def shift(t, g):
                if not has(t):
                    return
                first, n = GROUPS[g]
                wait(pool, max_ready, nth(t, 3, g))
                p = prob[:, HEADS * first:HEADS * (first + n), 0:NT]
                m = smax[:, HEADS * first:HEADS * (first + n)].unsqueeze(2).broadcast_to([128, HEADS * n, NT])
                pool.tensor_tensor(p, p, m, ALU.subtract).then_inc(shifted, 1)

            def divide(t, g):
                if not has(t):
                    return
                first, n = GROUPS[g]
                wait(pool, rec_ready, nth(t, 3, g))
                p = prob[:, HEADS * first:HEADS * (first + n), 0:NT]
                r = srec[:, HEADS * first:HEADS * (first + n)].unsqueeze(2).broadcast_to([128, HEADS * n, NT])
                pool.tensor_tensor(p, p, r, ALU.mult).then_inc(p_ready, 1)

            def root(which, s):
                b = ln[which]
                wait(pool, ln_ready[which], nth(s, 1, 0))
                pool.tensor_tensor(b["rstd"][:], b["var_eps"][:], minus_half[0:PT_], ALU.pow)\
                    .then_inc(rstd_done[which], 1)
                wait(pool, rstd_done[which], nth(s, 1, 0))
                pool.tensor_tensor(b["offset"][:], b["minus_mean"][:], b["rstd"][:], ALU.mult)\
                    .then_inc(scale_ready[which], 1)

            def step(t, phase):
                if has(t - 1):
                    root(1, t - 1)
                shift(t, 0)
                shift(t, 1)
                shift(t, 2)
                for g in range(3):
                    divide(t, g)
                if has(t + 2):
                    root(0, t + 2)

            steps(pool, step)


_F = "float32"
_BLOCK = "L0_conv_"
_CONV = "L1_conv_"
_INS = ([_BLOCK + n for n in ("qkv_w", "qkv_b", "proj_w", "proj_b", "rel_bias", "ln1_g", "ln1_b", "ln2_g", "ln2_b",
                              "fc1_w", "fc1_b", "fc2_w", "fc2_b")]
        + [_CONV + n for n in ("dw_kernel", "dw_bias", "pw_kernel", "pw_bias", "gamma", "beta", "moving_mean",
                               "moving_var")])


def constants():
    eye = np.eye(128, dtype=_F)
    rolled = np.zeros((PT_, PT_), _F)
    for r in range(WS):
        for w in range(NWIN):
            rolled[r * NWIN + (w + 1) % NWIN, r * NWIN + w] = 1.0
    col, row = np.arange(NT) // WS, np.arange(NT) % WS
    far_col, far_row = col >= WS - SHIFT, row >= WS - SHIFT
    apart_col = far_col[:, None] != far_col[None, :]
    apart_row = far_row[:, None] != far_row[None, :]
    mask = np.zeros((128, 2, 2, NT), _F)
    for last_strip in range(2):
        for last_pair in range(2):
            for side in range(2):
                apart = (apart_row if last_strip else np.zeros_like(apart_row)) | (
                    apart_col if last_pair and side else np.zeros_like(apart_col))
                mask[64 * side:64 * side + NT, last_strip, last_pair] = np.where(apart, MASKED, 0.0)
    blocks = np.zeros((128, 4, C), _F)
    blocks[0:64, :, 0:HD] = 1.0
    blocks[64:128, :, HD:2 * HD] = 1.0
    blocks[0:64, 0:2, 2 * HD:] = 1.0
    blocks[64:128, 2:4, 2 * HD:] = 1.0
    return {"eye": eye, "rolled_eye": rolled, "mask": mask, "head_blocks": blocks}


def kernel(**inputs):
    import concourse.bacc as bacc
    from concourse.bass_utils import run_bass_kernel_spmd

    nc = bacc.Bacc("TRN2", target_bir_lowering=False, num_devices=1)
    arrays, args = {}, []

    def give(name, a):
        a = np.ascontiguousarray(a)
        arrays[name] = a
        args.append(nc.dram_tensor(name, a.shape, mybir.dt.from_np(a.dtype), kind="ExternalInput").ap())

    give("in_x", inputs["x"])
    for name in _INS:
        a = np.asarray(inputs[name])
        if name.endswith("rel_bias"):
            side = 2 * WS - 1
            a = a.reshape(side, side, HEADS)[::-1, ::-1].transpose(2, 1, 0)
        elif name.endswith("qkv_b"):
            a = a.reshape(3, C).T
        elif name.endswith("fc1_b"):
            a = a.reshape(MC, 128).T
        elif name.endswith("dw_kernel"):
            a = a.reshape(9, C).T
        give("in_" + name, a)
    for name, a in constants().items():
        give("const_" + name, a)
    shape = tuple(inputs["x"].shape)
    args.append(nc.dram_tensor("out_0", shape, F32, kind="ExternalOutput").ap())
    swin_conv_kernel(nc, *args)
    r = run_bass_kernel_spmd(nc, [arrays], core_ids=[0])
    return r.results[0]["out_0"]
```

```python
from contextlib import ExitStack

import numpy as np

import concourse.bass as bass
from concourse import mybir

ALU = mybir.AluOpType
ACT = mybir.ActivationFunctionType
F32 = mybir.dt.float32
AX_X = mybir.AxisListType.X

WS, SHIFT = 7, 3
NT = WS * WS
HW, C, HEADS = 112, 96, 3
HD = C // HEADS
NWIN = HW // WS
TOK = WS * HW
PT_ = WS * NWIN
HALF = TOK // 2
HID = 4 * C
MC = HID // 128
PAIRS = NWIN // 2
GROUPS = [(0, 3), (3, 3), (6, 2)]
HEAD_ORDER = ((0, 1, 2), (2, 0, 1))
HALVES = ((0, 4), (4, 3))
SCALE = float(HD) ** -0.5
LN_EPS, BN_EPS = 1e-4, 1e-3
MASKED = -100.0

MAP_W = HW + 2
AREA = 10
AREAS = 5
TOP_ROWS, LOW_ROWS = 5, 2

ACT_NORM = 4
LOOP_FIRST = 6
KEYS = 4 * 16
UNROLL = 4


def swin_conv_kernel(nc, x, qkv_w, qkv_b, proj_w, proj_b, rel_bias_rt, ln1_g, ln1_b, ln2_g, ln2_b,
                     fc1_w, fc1_b, fc2_w, fc2_b, dw_kernel, dw_bias, pw_kernel, pw_bias, gamma, beta,
                     moving_mean, moving_var, eye, rolled_eye, mask, head_blocks, out):
    B = x.shape[0]
    NS = B * NWIN
    LOOPS = (NS - 3 - LOOP_FIRST) // UNROLL

    x_chunks = x.rearrange("b h (c j) f -> (b h c) (j f)", j=WS)
    out_rows = out.rearrange("b h w f -> (b h) w f")

    def nth(strip, tiles, tile):
        if isinstance(strip, int) and strip > NS - 1:
            return tiles * NS
        return tiles * strip + tile + 1

    def wait(eng, sem, count):
        if isinstance(count, int) and count <= 0:
            return
        eng.wait_ge(sem, count)

    def has(strip):
        return not isinstance(strip, int) or 0 <= strip < NS

    def start(value, most):
        if isinstance(value, int):
            return value
        return nc.s_assert_within(value, 0, most,
                                  skip_runtime_bounds_check_because="it follows from the strip's number")

    def steps(eng, step, first=-2):
        for t in range(first, LOOP_FIRST):
            step(t, t % UNROLL)
        with eng.Fori(0, LOOPS) as it:
            for u in range(UNROLL):
                step(it * UNROLL + (LOOP_FIRST + u), (LOOP_FIRST + u) % UNROLL)
        for t in range(LOOP_FIRST + UNROLL * LOOPS, NS + 4):
            step(t, t % UNROLL)

    def is_zero(value, period):
        return 1 - (value + period - 1) // period

    def area_of_strip(s):
        k = s % NWIN
        own = k % 2 + (k + 1) // NWIN + is_zero(s % (2 * NWIN), 2 * NWIN) * 3 \
            + is_zero((s + NWIN) % (2 * NWIN), 2 * NWIN) * 4
        return own * AREA

    def area_below_strip(s):
        k = (s + 1) % NWIN
        below = k % 2 + (k + 1) // NWIN + is_zero((s + 1) % (2 * NWIN), 2 * NWIN) * 4 \
            + is_zero((s + 1 + NWIN) % (2 * NWIN), 2 * NWIN) * 3
        return below * AREA

    with ExitStack() as ctx:
        def sb(name, *shape):
            return ctx.enter_context(nc.sbuf_tensor(name, list(shape), F32))

        def sem(name):
            return ctx.enter_context(nc.semaphore(name))

        ident = sb("ident", 128, 128)
        roll = sb("roll", PT_, PT_)
        heads = sb("heads", 128, 4, C)
        table = sb("table", 128, 2, PAIRS * HEADS, NT)
        wqkv = sb("wqkv", C, 2 * C + 4 * HD)
        wproj = sb("wproj", C + 1, C)
        w1 = sb("w1", C, HID)
        w2 = sb("w2", 128, MC, C)
        wpw = sb("wpw", C + 1, C)
        taps = sb("taps", C, 9)
        cols = sb("cols", C, 8)
        bqkv = sb("bqkv", C, 3)
        bfc1 = sb("bfc1", 128, MC)
        minus_half = sb("minus_half", 128, WS)
        table_load = sb("table_load", 1, 2)

        x_in = sb("x_in", PT_, 4, WS, C)
        xn = sb("xn", PT_, WS, C)
        x1 = sb("x1", PT_, WS, C)
        x1n = sb("x1n", PT_, WS, C)
        o_tile = sb("o_tile", HW, 2, WS, C)
        xT = sb("xT", C, NWIN, 64)
        qT = sb("qT", C, TOK + 16)
        kT = sb("kT", C, TOK)
        kbd = sb("kbd", C, HEADS + 1, TOK)
        prob = sb("prob", 128, PAIRS * HEADS, 64)
        vbd = sb("vbd", 128, 2, NWIN * C)
        probT = sb("probT", 128, 4, 3, 128)
        attnT = sb("attnT", C + 1, NT, NWIN)
        x1T = sb("x1T", C, TOK)
        hT = sb("hT", 128, MC, TOK)
        acc = sb("acc", C + 1, 2, WS, HW)
        ymap = sb("ymap", C, AREAS * AREA, MAP_W)
        smax = sb("smax", 128, PAIRS * HEADS)
        ssum = sb("ssum", 128, PAIRS * HEADS)
        srec = sb("srec", 128, PAIRS * HEADS)
        ln = [{name: sb(f"{name}{i}", PT_, *shape) for name, shape in
               (("stats", (WS, 6)), ("sum", (WS,)), ("diff", (WS,)), ("dev", (WS,)), ("between", (WS,)),
                ("within", (WS,)), ("minus_mean", (WS,)), ("var_eps", (WS,)), ("rstd", (WS,)),
                ("offset", (WS,)))} for i in (1, 2)]

        bank = [ctx.enter_context(nc.psum_tensor(f"bank{i}", [128, 512], F32)) for i in range(8)]

        const_loaded, rows_loaded = sem("const_loaded"), sem("rows_loaded")
        bias_loaded, bias_doubled, row_moved = sem("bias_loaded"), sem("bias_doubled"), sem("row_moved")
        pool_cleared, dve_set, pe_set, pool_set = sem("pool_cleared"), sem("dve_set"), sem("pe_set"), sem("pool_set")
        x_loaded = [sem(f"x_loaded{i}") for i in range(4)]
        out_stored = [sem(f"out_stored{i}") for i in range(2)]
        k_ready = sem("k_ready")
        xt_psum, q_psum, k_psum, v_psum = sem("xt_psum"), sem("q_psum"), sem("k_psum"), sem("v_psum")
        s_psum, pt_psum, o_psum, proj_psum = sem("s_psum"), sem("pt_psum"), sem("o_psum"), sem("proj_psum")
        x1t_psum, h_psum, y_psum, yt_psum = sem("x1t_psum"), sem("h_psum"), sem("y_psum"), sem("yt_psum")
        pw_psum = sem("pw_psum")
        xt_ready, q_ready, k_copied, exp_done = sem("xt_ready"), sem("q_ready"), sem("k_copied"), sem("exp_done")
        pt_ready, o_ready, x1t_ready = sem("pt_ready"), sem("o_ready"), sem("x1t_ready")
        h_ready, ymap_ready, out_ready = sem("h_ready"), sem("ymap_ready"), sem("out_ready")
        xn_ready, x1n_ready = sem("xn_ready"), sem("x1n_ready")
        s_biased, max_ready, sum_done, rec_ready = sem("s_biased"), sem("max_ready"), sem("sum_done"), sem("rec_ready")
        v_ready, y_ready, x1_ready = sem("v_ready"), sem("y_ready"), sem("x1_ready")
        stats_done = [sem("stats1_done"), sem("stats2_done")]
        parts_done = [sem("parts1_done"), sem("parts2_done")]
        halves_done = [sem("halves1_done"), sem("halves2_done")]
        ln_ready = [sem("ln1_ready"), sem("ln2_ready")]
        top_done, low_done = sem("top_done"), sem("low_done")
        shifted, p_ready = sem("shifted"), sem("p_ready")
        rstd_done = [sem("rstd1_done"), sem("rstd2_done")]
        scale_ready = [sem("scale1_ready"), sem("scale2_ready")]
        xn_rest, x1n_rest = sem("xn_rest"), sem("x1n_rest")

        bias0 = hT[:, 0, 0:HEADS * NT]
        maskt = hT[:, 1, 0:4 * NT].rearrange("p (a b m) -> p a b m", a=2, b=2)
        pw_raw = hT[0:C, 2, 0:C]
        qkv_raw = hT[0:C, 2, C:4 * C]
        proj_row = hT[0:1, 2, 4 * C:5 * C]
        w1_raw = x1T[:, 0:HID]
        rows = x1[0:1].rearrange("p j f -> p (j f)")
        proj_b_row, pw_b_row, gamma_row, beta_row, mean_row, var_row, one_row = (
            rows[:, i * C:(i + 1) * C] for i in range(7))
        scratch = x1n[0:1].rearrange("p j f -> p (j f)")
        inv_row, var_eps, row_a, row_b, pw_row, std_row, mh_row = (scratch[:, i * C:(i + 1) * C] for i in range(7))

        block = ctx.enter_context(nc.Block())

        @block.sync
        def _(sp):
            const = [
                (ident[:], eye), (roll[:], rolled_eye), (heads[:], head_blocks), (maskt, mask),
                (qkv_raw, qkv_w), (wproj[0:C], proj_w), (w1_raw, fc1_w),
                (w2[:], fc2_w.rearrange("(m p) n -> p m n", p=128)),
                (pw_raw, pw_kernel.rearrange("a b i o -> (a b i) o")),
                (taps[:], dw_kernel),
                (bqkv[:], qkv_b),
                (bfc1[:], fc1_b),
            ] + [(cols[:, i:i + 1], v.rearrange("(f u) -> f u", u=1))
                 for i, v in enumerate((ln1_g, ln1_b, ln2_g, ln2_b, fc2_b, dw_bias))]
            for dst, src in const:
                sp.dma_start(dst, src).then_inc(const_loaded, 16)
            for dst, src in ((proj_b_row, proj_b), (pw_b_row, pw_bias), (gamma_row, gamma), (beta_row, beta),
                             (mean_row, moving_mean), (var_row, moving_var)):
                sp.dma_start(dst, src.rearrange("(u f) -> u f", u=1)).then_inc(rows_loaded, 16)

            def load(t, phase):
                s = t + 3
                if not has(s):
                    return
                slot = (phase + 3) % UNROLL
                wait(sp, x1_ready, nth(t - 1, 2, 1))
                image, k = s // NWIN, s % NWIN
                first = (image * HW + k * WS + SHIFT) * NWIN
                wrapped = (image * HW + (k + 1) % NWIN * WS) * NWIN
                top = (WS - SHIFT) * NWIN
                dst = x_in[:, slot].rearrange("p j f -> p (j f)")
                sp.dma_start(dst[0:top], x_chunks[bass.ds(start(first, B * HW * NWIN - top), top)]).then_inc(x_loaded[slot], 16)
                sp.dma_start(dst[top:PT_], x_chunks[bass.ds(start(wrapped, B * HW * NWIN - (PT_ - top)), PT_ - top)]).then_inc(x_loaded[slot], 16)

            def spread_keys(t):
                if not has(t + 1):
                    return
                wait(sp, s_psum, nth(t, 3, 2))
                wait(sp, k_copied, nth(t + 1, 2, 1))
                for h, part in ((0, 1), (1, 2), (2, 0), (2, 3)):
                    hp = slice(h * HD, (h + 1) * HD)
                    sp.dma_start(kbd[hp, part, :], kT[hp, :]).then_inc(k_ready, 16)

            def store(t, phase):
                i = t - 4
                if not has(i):
                    return
                slot = phase % 2
                wait(sp, out_ready, nth(i, 2, 1))
                image, k = i // NWIN, (i + 1) % NWIN
                top = image * HW + k * WS + 2
                low = image * HW + (k + 1) % NWIN * WS
                for row, at, n in ((top, 0, TOP_ROWS), (low, TOP_ROWS, LOW_ROWS)):
                    sp.dma_start(out_rows[bass.ds(start(row, B * HW - n), n)].rearrange("r w f -> w r f"),
                                 o_tile[:, slot, at:at + n]).then_inc(out_stored[slot], 16)

            def step(t, phase):
                load(t, phase)
                spread_keys(t)
                store(t, phase)

            sp.wait_ge(pool_cleared, 1)
            side = 2 * WS - 1
            for jx in range(WS):
                for ry in range(WS):
                    n = jx * WS + ry
                    src = rel_bias_rt[:, WS - 1 - jx:side - jx, WS - 1 - ry:side - ry]
                    sp.dma_start(bias0[n:n + 1], src).then_inc(bias_loaded, 16)
            load(-3, 1)
            sp.wait_ge(bias_loaded, 16 * NT)
            sp.dma_start(bias0[64:64 + NT], bias0[0:NT]).then_inc(bias_doubled, 16)
            sp.wait_ge(dve_set, 6)
            sp.dma_start(wproj[C:C + 1], proj_row).then_inc(row_moved, 16)
            sp.wait_ge(dve_set, 12)
            sp.dma_start(wpw[C:C + 1], pw_row).then_inc(row_moved, 16)

            sp.wait_ge(pool_cleared, 2)
            steps(sp, step)
            stores = [(NS + 1) // 2, NS // 2]
            sp.wait_ge(out_stored[1], 32 * stores[0])
            sp.wait_ge(out_stored[0], 32 * stores[1])

        @block.tensor
        def _(pe):
            pe.wait_ge(const_loaded, 16 * 18)
            pe.wait_ge(rows_loaded, 16 * 6)
            for i in range(3):
                pe.matmul(bank[0][0:C, i:i + 1], qkv_raw[:, i * C:(i + 1) * C], cols[:, 1:2], start=True, stop=True)
            for m in range(MC):
                pe.matmul(bank[1][:, m:m + 1], w1_raw[:, m * 128:(m + 1) * 128], cols[:, 3:4], start=True, stop=True)
            pe.matmul(bank[2][0:1, 0:C], cols[:, 5:6], pw_raw, start=True, stop=True).then_inc(pe_set, 1)
            pe.wait_ge(dve_set, 3)
            pe.matmul(bank[3][0:1, 0:C], bqkv[:, 2:3], wproj[0:C], start=True, stop=True).then_inc(pe_set, 1)
            pe.wait_ge(dve_set, 9)
            pe.matmul(bank[4][0:C, 0:C], one_row, inv_row, start=True, stop=True).then_inc(pe_set, 1)
            pe.wait_ge(dve_set, 14)
            pe.wait_ge(row_moved, 32)
            pe.wait_ge(pool_cleared, 2)

            def scores(t):
                if not has(t):
                    return
                wait(pe, q_ready, nth(t, 2, 1))
                wait(pe, k_ready, KEYS * nth(t, 1, 0))
                for g, (first, n) in enumerate(GROUPS):
                    if g == 0:
                        wait(pe, xt_ready, nth(t + 1, 2, 1))
                    elif g == 1:
                        wait(pe, y_ready, nth(t - 2, 2, 1))
                    else:
                        wait(pe, ymap_ready, nth(t - 2, 2, 1))
                    for p in range(n):
                        for side in range(2):
                            w = 2 * (first + p) + side
                            mm = pe.matmul(bank[g][64 * side:64 * side + 64, p * HEADS * NT:(p + 1) * HEADS * NT],
                                           qT[:, w * NT:w * NT + 64],
                                           kbd[:, 1 - (first + p) % 2:4 - (first + p) % 2, w * NT:(w + 1) * NT],
                                           start=True, stop=True)
                    mm.then_inc(s_psum, 1)

            def queries_keys(t):
                if not has(t + 1):
                    return
                wait(pe, xt_ready, nth(t + 1, 2, 1))
                for u in range(2):
                    if u == 0:
                        wait(pe, pt_ready, nth(t - 1, 4, 1))
                    else:
                        wait(pe, ymap_ready, nth(t - 2, 2, 0))
                    pe.matmul(bank[3 + u][0:C, 0:HALF], wqkv[:, 0:C], xT[:, 8 * u:8 * u + 8, 0:NT],
                              start=True, stop=True).then_inc(q_psum, 1)
                for u in range(2):
                    if u == 0:
                        wait(pe, x1_ready, nth(t - 1, 2, 0))
                    else:
                        wait(pe, o_ready, nth(t - 1, 2, 1))
                    pe.matmul(bank[5 + u][0:C, 0:HALF], wqkv[:, C:2 * C], xT[:, 8 * u:8 * u + 8, 0:NT],
                              start=True, stop=True).then_inc(k_psum, 1)

            def values(t, tiles):
                if not has(t + 1):
                    return
                for i in tiles:
                    wait(pe, s_biased, nth(t, 3, i + 1))
                    for j in range(8):
                        for side in range(2):
                            rhs = wqkv[:, 2 * C + side * 2 * HD:2 * C + (side + 1) * 2 * HD]
                            mm = pe.matmul(bank[1 + i][64 * side:64 * side + 64, j * 2 * HD:(j + 1) * 2 * HD],
                                           xT[:, 8 * i + j], rhs, start=True, stop=True)
                    mm.then_inc(v_psum, 1)

            def turn_x1(t):
                if not has(t - 1):
                    return
                wait(pe, x1n_ready, nth(t - 1, 1, 0))
                wait(pe, x1n_rest, nth(t - 1, 1, 0))
                for i, (js, b) in enumerate(((range(0, 4), 7), (range(4, 7), 0))):
                    if i == 0:
                        wait(pe, x1_ready, nth(t - 1, 2, 1))
                    else:
                        wait(pe, s_biased, nth(t, 3, 0))
                    for a, j in enumerate(js):
                        mm = pe.transpose(bank[b][0:C, a * PT_:(a + 1) * PT_], x1n[:, j, :], ident[0:PT_, 0:PT_])
                    mm.then_inc(x1t_psum, 1)

            def hidden(t, half):
                if not has(t - 1):
                    return
                for i in range(MC * half, MC * (half + 1)):
                    m = i % MC
                    first, n = ((0, 4), (4, 3))[half]
                    if m == 0:
                        wait(pe, x1t_ready, nth(t - 1, 2, half))
                    if i < 2:
                        wait(pe, k_copied, nth(t + 1, 2, i))
                    elif i == 2:
                        wait(pe, x1t_ready, nth(t - 1, 2, 0))
                    else:
                        wait(pe, h_ready, nth(t - 1, 6, i - 3))
                    pe.matmul(bank[5 + i % 3][:, 0:n * PT_], w1[:, m * 128:(m + 1) * 128],
                              x1T[:, first * PT_:(first + n) * PT_], start=True, stop=True).then_inc(h_psum, 1)

            def second_layer(t):
                if not has(t - 1):
                    return
                for half, (first, n) in enumerate(((0, 4), (4, 3))):
                    wait(pe, h_ready, nth(t - 1, 6, 3 * half + 2))
                    if half == 0:
                        wait(pe, x1t_ready, nth(t - 1, 2, 1))
                    else:
                        wait(pe, v_ready, nth(t + 1, 2, 0))
                        wait(pe, s_biased, nth(t, 3, 1))
                    for a in range(n):
                        j = first + a
                        for m in range(MC):
                            mm = pe.matmul(bank[half][0:PT_, a * C:(a + 1) * C], hT[:, m, j * PT_:(j + 1) * PT_],
                                           w2[:, m, :], start=(m == 0), stop=(m == MC - 1))
                    mm.then_inc(y_psum, 1)

            def turn_probs(t, d):
                wait(pe, p_ready, nth(t, 3, (2 * d + 1) // 3))
                if d == 0:
                    wait(pe, v_ready, nth(t + 1, 2, 1))
                elif d < 3:
                    wait(pe, q_ready, nth(t + 1, 2, d - 1))
                    wait(pe, out_ready, nth(t - 4, 2, d - 1))
                else:
                    wait(pe, pt_ready, nth(t, 4, 0))
                b = bank[(2, 3, 4, 2)[d]]
                for i, slot in enumerate((0, 4, 2)):
                    mm = pe.transpose(b[:, i * 128:(i + 1) * 128], prob[:, 6 * d + slot:6 * d + slot + 2, :], ident[:])
                mm.then_inc(pt_psum, 1)

            def weigh_values(t, phase, d):
                if d == 0:
                    wait(pe, v_ready, nth(t, 2, 1))
                    wait(pe, h_ready, nth(t - 1, 6, 3))
                if d == 2:
                    wait(pe, h_ready, nth(t - 1, 6, 4))
                wait(pe, pt_ready, nth(t, 4, d))
                b, v = bank[5 + d // 2], vbd[:, phase % 2]
                for j in range(4):
                    w = 4 * d + j
                    at = (w % 8) * NT
                    side = 64 * (j % 2)
                    for h in range(HEADS):
                        mm = pe.matmul(b[h * HD:(h + 1) * HD, at:at + NT], v[:, w * C + h * HD:w * C + (h + 1) * HD],
                                       probT[:, d, j // 2 if h < 2 else 2, side:side + NT], start=True, stop=True)
                if d % 2:
                    mm.then_inc(o_psum, 1)

            def turn_x(t, i):
                if not has(t + 2):
                    return
                wait(pe, xn_ready, nth(t + 2, 1, 0))
                wait(pe, xn_rest, nth(t + 2, 1, 0))
                js, perm, b = ((range(3, 7), ident[0:PT_, 0:PT_], 7), (range(0, 3), roll[:], 0))[i]
                if i == 0:
                    wait(pe, h_ready, nth(t - 1, 6, 5))
                else:
                    wait(pe, y_ready, nth(t - 1, 2, 0))
                for a, j in enumerate(js):
                    mm = pe.transpose(bank[b][0:C, a * PT_:(a + 1) * PT_], xn[:, j, :], perm)
                mm.then_inc(xt_psum, 1)

            def pointwise(t, phase):
                if not has(t - 4):
                    return
                wait(pe, top_done, nth(t - 4, 9, 8))
                wait(pe, low_done, nth(t - 4, 9, 8))
                for i, ((first, n), b) in enumerate(zip(HALVES, (3, 4))):
                    wait(pe, q_ready, nth(t + 1, 2, i))
                    wait(pe, ymap_ready, nth(t - 2, 2, 1))
                    wait(pe, out_ready, nth(t - 5, 2, i))
                    for a in range(n):
                        mm = pe.matmul(bank[b][0:HW, a * C:(a + 1) * C], acc[:, phase % 2, first + a, :], wpw[:],
                                       start=True, stop=True)
                    mm.then_inc(pw_psum, 1)

            def turn_y(t):
                if not has(t - 1):
                    return
                for i, (first, n, b) in enumerate(((0, 4, 4), (4, 3, 2))):
                    wait(pe, y_ready, nth(t - 1, 2, i))
                    wait(pe, pt_ready, nth(t, 4, i + 2))
                    if i == 0:
                        wait(pe, out_ready, nth(t - 4, 2, 1))
                    for a in range(n):
                        mm = pe.transpose(bank[b][0:C, a * PT_:(a + 1) * PT_], x1[:, first + a, :],
                                          ident[0:PT_, 0:PT_])
                    mm.then_inc(yt_psum, 1)

            def project(t):
                if not has(t):
                    return
                wait(pe, o_ready, nth(t, 2, 1))
                for i, (first, n, b) in enumerate(((0, 4, 5), (4, 3, 7))):
                    if i == 1:
                        wait(pe, xt_ready, nth(t + 2, 2, 0))
                    for a in range(n):
                        j = first + a
                        col = j - SHIFT if j >= SHIFT else j - SHIFT + WS
                        mm = pe.matmul(bank[b][0:PT_, a * C:(a + 1) * C],
                                       attnT[:, col * WS:(col + 1) * WS, :], wproj[:],
                                       start=True, stop=True)
                    mm.then_inc(proj_psum, 1)

            def step(t, phase):
                scores(t)
                queries_keys(t)
                values(t, (0,))
                turn_x1(t)
                values(t, (1,))
                hidden(t, 0)
                hidden(t, 1)
                pointwise(t, phase)
                second_layer(t)
                turn_x(t, 0)
                if has(t):
                    for d in range(3):
                        turn_probs(t, d)
                turn_x(t, 1)
                if has(t):
                    weigh_values(t, phase, 0)
                    turn_probs(t, 3)
                    for d in range(1, 4):
                        weigh_values(t, phase, d)
                turn_y(t)
                project(t)

            steps(pe, step)

        @block.scalar
        def _(act):
            act.wait_ge(dve_set, 14)
            act.wait_ge(pool_cleared, 2)

            def exps(t, g):
                if not has(t):
                    return
                first, n = GROUPS[g]
                wait(act, shifted, nth(t, 3, g))
                p = prob[:, HEADS * first:HEADS * (first + n), 0:NT]
                act.activation(p, p, ACT.Exp).then_inc(exp_done, 1)

            def queries(t):
                if not has(t + 1):
                    return
                wait(act, s_psum, nth(t, 3, 2))
                for u in range(2):
                    wait(act, q_psum, nth(t + 1, 2, u))
                    act.activation(qT[:, u * HALF:(u + 1) * HALF], bank[3 + u][0:C, 0:HALF], ACT.Identity,
                                   bias=bqkv[:, 0:1], scale=SCALE).then_inc(q_ready, 1)

            def keys(t):
                if not has(t + 1):
                    return
                wait(act, k_ready, KEYS * nth(t, 1, 0))
                for u in range(2):
                    wait(act, k_psum, nth(t + 1, 2, u))
                    act.activation(kT[:, u * HALF:(u + 1) * HALF], bank[5 + u][0:C, 0:HALF], ACT.Identity,
                                   bias=bqkv[:, 1:2]).then_inc(k_copied, 1)

            def outputs(t, phase):
                if not has(t - 4):
                    return
                slot = phase % 2
                wait(act, out_stored[slot], 32 * ((t - 4) // 2))
                for i, ((first, n), b) in enumerate(zip(HALVES, (3, 4))):
                    wait(act, pw_psum, nth(t - 4, 2, i))
                    act.copy(o_tile[:, slot, first:first + n],
                             bank[b][0:HW, 0:n * C].rearrange("p (r f) -> p r f", r=n)).then_inc(out_ready, 1)

            def normalise(which, s, dst, src, ready):
                b = ln[which]
                wait(act, scale_ready[which], nth(s, 1, 0))
                for j in range(ACT_NORM):
                    last = act.activation(dst[:, j], src[:, j], ACT.Identity, bias=b["offset"][:, j:j + 1],
                                          scale=b["rstd"][:, j:j + 1])
                last.then_inc(ready, 1)

            def x1_turned(t):
                if not has(t - 1):
                    return
                wait(act, h_psum, nth(t - 2, 6, 5))
                for i, (first, n, b) in enumerate(((0, 4, 7), (4, 3, 0))):
                    wait(act, x1t_psum, nth(t - 1, 2, i))
                    act.copy(x1T[:, first * PT_:(first + n) * PT_], bank[b][0:C, 0:n * PT_]).then_inc(x1t_ready, 1)

            def gelus(t):
                if not has(t - 1):
                    return
                act.activation(table_load[:, 1:2], table_load[:, 0:1], ACT.Gelu_apprx_tanh)
                wait(act, y_psum, nth(t - 2, 2, 1))
                for i in range(2 * MC):
                    half, m = i // MC, i % MC
                    first, n = ((0, 4), (4, 3))[half]
                    wait(act, h_psum, nth(t - 1, 6, i))
                    act.activation(hT[:, m, first * PT_:(first + n) * PT_], bank[5 + i % 3][:, 0:n * PT_],
                                   ACT.Gelu_apprx_tanh, bias=bfc1[:, m:m + 1]).then_inc(h_ready, 1)

            def probs_turned(t, tiles):
                if not has(t):
                    return
                wait(act, o_psum, nth(t - 1, 2, 1))
                for d in tiles:
                    wait(act, pt_psum, nth(t, 4, d))
                    act.copy(probT[:, d].rearrange("p i n -> p (i n)"), bank[(2, 3, 4, 2)[d]][:, 0:384])\
                        .then_inc(pt_ready, 1)

            def attention_out(t):
                if not has(t):
                    return
                wait(act, proj_psum, nth(t - 1, 2, 1))
                far = (WS - SHIFT) * WS
                for u in range(2):
                    wait(act, o_psum, nth(t, 2, u))
                    src = bank[5 + u][0:C, 0:8 * NT].rearrange("p (w n) -> p w n", w=8)
                    dst = attnT[0:C].rearrange("p n w -> p w n")
                    act.copy(dst[:, 8 * u:8 * u + 8, 0:far], src[:, :, 0:far])
                    inner = 8 - u
                    last = act.copy(dst[:, 8 * u + 1:8 * u + 1 + inner, far:], src[:, 0:inner, far:])
                    if u == 1:
                        last = act.copy(dst[:, 0, far:], src[:, 7, far:])
                    last.then_inc(o_ready, 1)

            def x_turned(t, i):
                if not has(t + 2):
                    return
                first, n, b = ((0, 4, 7), (4, 3, 0))[i]
                wait(act, v_psum, nth(t + 1, 2, 1))
                wait(act, xt_psum, nth(t + 2, 2, i))
                src = bank[b][0:C, 0:n * PT_].rearrange("p (n w) -> p n w", w=NWIN)
                dst = xT[:].rearrange("p w n -> p n w")[:, first * WS:(first + n) * WS, :]
                act.copy(dst, src).then_inc(xt_ready, 1)

            def into_map(t, phase):
                if not has(t - 1):
                    return
                s = t - 1
                wait(act, top_done, nth(t - 3, 9, 8))
                wait(act, low_done, nth(t - 3, 9, 8))
                area = area_of_strip(s)
                if phase == 0:
                    parts = [(0, 4, area + 2), (4, 3, area + 6 + (s % NWIN + 1) // NWIN)]
                else:
                    parts = [(0, 7, area + 2)]
                parts.append((5, 2, area_below_strip(s)))
                for i, ((first, n), b) in enumerate(zip(HALVES, (4, 2))):
                    wait(act, yt_psum, nth(s, 2, i))
                    src = bank[b][0:C, 0:n * PT_].rearrange("p (j r c) -> p j r c", j=n, r=WS)
                    for r0, nr, row in parts:
                        dst = ymap[:, bass.ds(start(row, AREAS * AREA - nr), nr), 1:1 + HW].rearrange("p r (c j) -> p j r c", j=WS)
                        last = act.activation(dst[:, first:first + n], src[:, :, r0:r0 + nr, :], ACT.Relu,
                                              bias=cols[:, 4:5])
                    last.then_inc(ymap_ready, 1)

            def step(t, phase):
                queries(t)
                if has(t - 1):
                    wait(act, x1t_psum, nth(t - 2, 2, 1))
                    normalise(1, t - 1, x1n, x1, x1n_ready)
                keys(t)
                x1_turned(t)
                gelus(t)
                for g in range(3):
                    exps(t, g)
                if has(t + 2):
                    wait(act, xt_psum, nth(t + 1, 2, 1))
                    normalise(0, t + 2, xn, x_in[:, (phase + 2) % UNROLL], xn_ready)
                outputs(t, phase)
                probs_turned(t, range(0, 3))
                x_turned(t, 0)
                probs_turned(t, range(3, 4))
                x_turned(t, 1)
                attention_out(t)
                into_map(t, phase)

            steps(act, step)

        @block.vector
        def _(dve):
            dve.memset(attnT[C:C + 1], 1.0)
            dve.memset(acc[C:C + 1], 1.0)
            dve.memset(one_row, 1.0).then_inc(dve_set, 1)
            dve.wait_ge(const_loaded, 16 * 18)
            dve.wait_ge(rows_loaded, 16 * 6)
            dve.wait_ge(pe_set, 1)
            dve.tensor_tensor(bfc1[:], bank[1][:, 0:MC], bfc1[:], ALU.add).then_inc(dve_set, 1)
            dve.tensor_tensor(bqkv[:], bank[0][0:C, 0:3], bqkv[:], ALU.add).then_inc(dve_set, 1)
            dve.wait_ge(dve_set, 3)
            dve.tensor_scalar(bqkv[:, 0:1], bqkv[:, 0:1], SCALE, None, ALU.mult).then_inc(dve_set, 1)
            dve.tensor_scalar(wqkv[:, 0:2 * C], qkv_raw[:, 0:2 * C], cols[:, 0:1], None, ALU.mult)
            raw_heads = qkv_raw[:, 2 * C:3 * C].rearrange("p (h f) -> p h f", h=HEADS)
            v_heads = wqkv[:, 2 * C:].rearrange("p (h f) -> p h f", h=4)
            dve.tensor_scalar(v_heads[:, 0:2], raw_heads[:, 0:3:2], cols[:, 0:1], None, ALU.mult)
            dve.tensor_scalar(v_heads[:, 2:4], raw_heads[:, 1:3], cols[:, 0:1], None, ALU.mult)\
                .then_inc(dve_set, 1)
            dve.wait_ge(pe_set, 2)
            dve.tensor_tensor(proj_row, bank[3][0:1, 0:C], proj_b_row, ALU.add).then_inc(dve_set, 1)
            dve.tensor_scalar(w1[:], w1_raw, cols[:, 2:3], None, ALU.mult).then_inc(dve_set, 1)
            dve.tensor_scalar(var_eps, var_row, BN_EPS, None, ALU.add).then_inc(dve_set, 1)
            dve.wait_ge(pool_set, 1)
            dve.tensor_tensor(inv_row, std_row, gamma_row, ALU.mult).then_inc(dve_set, 1)
            dve.tensor_tensor(row_a, bank[2][0:1, 0:C], pw_b_row, ALU.add).then_inc(dve_set, 1)
            dve.wait_ge(dve_set, 10)
            dve.tensor_tensor(row_b, row_a, mean_row, ALU.subtract).then_inc(dve_set, 1)
            dve.wait_ge(dve_set, 11)
            dve.tensor_tensor(row_a, row_b, inv_row, ALU.mult).then_inc(row_step := sem("row_step"), 1)
            dve.wait_ge(row_step, 1)
            dve.tensor_tensor(pw_row, row_a, beta_row, ALU.add).then_inc(dve_set, 1)
            dve.wait_ge(pe_set, 3)
            dve.tensor_tensor(wpw[0:C], bank[4][0:C, 0:C], pw_raw, ALU.mult).then_inc(dve_set, 1)
            dve.wait_ge(bias_doubled, 16)
            for last_strip in range(2):
                for p in range(PAIRS):
                    m = maskt[:, last_strip, p // (PAIRS - 1)]
                    for i, h in enumerate(HEAD_ORDER[p % 2]):
                        last = dve.tensor_tensor(table[:, last_strip, HEADS * p + i], bias0[:, h * NT:(h + 1) * NT],
                                                 m, ALU.add)
            last.then_inc(dve_set, 1)
            dve.wait_ge(dve_set, 14)
            dve.wait_ge(pool_cleared, 2)
            dve.wait_ge(row_moved, 32)

            def add_bias(t, phase, g):
                if not has(t):
                    return
                first, n = GROUPS[g]
                if g == 0:
                    wait(dve, pt_psum, nth(t - 1, 4, 3))
                wait(dve, s_psum, nth(t, 3, g))
                which = (t % NWIN + 1) // NWIN if phase == UNROLL - 1 else 0
                bias = (table[:, which] if isinstance(which, int) else table[:, bass.ds(start(which, 1), 1)].squeeze(1))
                dst = prob[:, HEADS * first:HEADS * (first + n), 0:NT]
                dve.tensor_tensor(dst,
                                  bank[g][:, 0:n * HEADS * NT].rearrange("p (a m) -> p a m", m=NT),
                                  bias[:, HEADS * first:HEADS * (first + n)],
                                  ALU.add).then_inc(s_biased, 1)

            def find_max(t, g):
                if not has(t):
                    return
                first, n = GROUPS[g]
                at = slice(HEADS * first, HEADS * (first + n))
                wait(dve, s_biased, nth(t, 3, g))
                dve.tensor_reduce(smax[:, at], prob[:, at, 0:NT], AX_X, ALU.max).then_inc(max_ready, 1)

            def add_up(t, g):
                if not has(t):
                    return
                first, n = GROUPS[g]
                at = slice(HEADS * first, HEADS * (first + n))
                wait(dve, exp_done, nth(t, 3, g))
                p = prob[:, HEADS * first:HEADS * (first + n), 0:NT]
                dve.tensor_reduce(ssum[:, at], p, AX_X, ALU.add).then_inc(sum_done, 1)
                wait(dve, sum_done, nth(t, 3, g))
                dve.reciprocal(srec[:, at], ssum[:, at]).then_inc(rec_ready, 1)

            def tap(t, phase, i):
                c = t - 3
                if not has(c):
                    return
                dy, dx = i // 3 - 1, i % 3
                top = area_below_strip(c) + 1 + dy
                low = top + TOP_ROWS + ((c + 1) % NWIN + 1) // NWIN
                if i == 0:
                    wait(dve, ymap_ready, nth(c + 1, 2, 1))
                    wait(dve, pw_psum, nth(t - 5, 2, 1))
                for row, at, n, done in ((top, 0, TOP_ROWS, top_done), (low, TOP_ROWS, LOW_ROWS, low_done)):
                    src = ymap[:, bass.ds(start(row, AREAS * AREA - n), n), dx:dx + HW]
                    dst = acc[0:C, (phase + 1) % 2, at:at + n, :]
                    if i == 0:
                        dve.tensor_scalar(dst, src, taps[:, 0:1], None, ALU.mult).then_inc(done, 1)
                    else:
                        wait(dve, done, nth(c, 9, i - 1))
                        dve.scalar_tensor_tensor(out=dst, in0=src, scalar=taps[:, i:i + 1], in1=dst,
                                                 op0=ALU.mult, op1=ALU.add).then_inc(done, 1)

            def values(t, phase, i):
                if not has(t + 1):
                    return
                wait(dve, o_psum, nth(t - 1, 2, 1))
                wait(dve, v_psum, nth(t + 1, 2, i))
                src = bank[1 + i][:].rearrange("p (g w h f) -> p g w h f", g=2, w=4, h=2)
                dst = vbd[:, (phase + 1) % 2, 8 * i * C:8 * (i + 1) * C].rearrange(
                    "p (g w h f) -> p g w h f", g=2, w=4, h=HEADS)
                dve.tensor_tensor(dst[:, :, :, 0:2].rearrange("p g w h f -> p (g w) h f"),
                                  src[:, :, :, 0].rearrange("p g w f -> p (g w) f").unsqueeze(2).broadcast_to([128, 8, 2, HD]),
                                  heads[:, 0, 0:2 * HD].rearrange("p (h f) -> p h f", h=2).unsqueeze(1).broadcast_to([128, 8, 2, HD]),
                                  ALU.mult)
                dve.tensor_tensor(dst[:, :, :, 2], src[:, :, :, 1],
                                  heads[:, :, 2 * HD:].unsqueeze(1).broadcast_to([128, 2, 4, HD]),
                                  ALU.mult).then_inc(v_ready, 1)

            def norm_stats(which, s, src, eps):
                b = ln[which]
                for j in range(WS):
                    last = dve.bn_stats(b["stats"][:, j], src[:, j])
                last.then_inc(stats_done[which], 1)
                st = b["stats"]
                wait(dve, stats_done[which], nth(s, 1, 0))
                dve.tensor_tensor(b["sum"][:], st[:, :, 1], st[:, :, 4], ALU.add)
                dve.tensor_tensor(b["diff"][:], st[:, :, 1], st[:, :, 4], ALU.subtract)
                dve.tensor_tensor(b["dev"][:], st[:, :, 2], st[:, :, 5], ALU.add).then_inc(parts_done[which], 1)
                wait(dve, parts_done[which], nth(s, 1, 0))
                dve.tensor_scalar(b["minus_mean"][:], b["sum"][:], -0.5, None, ALU.mult)
                dve.scalar_tensor_tensor(out=b["between"][:], in0=b["diff"][:], scalar=0.25, in1=b["diff"][:],
                                         op0=ALU.mult, op1=ALU.mult)
                dve.tensor_scalar(b["within"][:], b["dev"][:], 1.0 / C, eps, ALU.mult, ALU.add)\
                    .then_inc(halves_done[which], 1)
                wait(dve, halves_done[which], nth(s, 1, 0))
                dve.tensor_tensor(b["var_eps"][:], b["between"][:], b["within"][:], ALU.add)\
                    .then_inc(ln_ready[which], 1)

            def norm_x(t, phase):
                if not has(t + 2):
                    return
                slot = (phase + 2) % UNROLL
                wait(dve, xn_ready, nth(t + 1, 1, 0))
                wait(dve, xn_rest, nth(t + 1, 1, 0))
                wait(dve, x_loaded[slot], 32 * ((t + 2) // UNROLL + 1))
                norm_stats(0, t + 2, x_in[:, slot], LN_EPS)

            def add_x1(t):
                if not has(t - 1):
                    return
                wait(dve, x1n_ready, nth(t - 1, 1, 0))
                wait(dve, x1n_rest, nth(t - 1, 1, 0))
                wait(dve, x1_ready, nth(t - 1, 2, 1))
                for i, (first, n) in enumerate(((0, 4), (4, 3))):
                    wait(dve, y_psum, nth(t - 1, 2, i))
                    js = slice(first, first + n)
                    dve.tensor_tensor(x1[:, js], bank[i][0:PT_, 0:n * C].rearrange("p (j f) -> p j f", j=n),
                                      x1[:, js], ALU.add).then_inc(y_ready, 1)

            def add_x(t, phase):
                if not has(t):
                    return
                wait(dve, yt_psum, nth(t - 1, 2, 1))
                for i, (first, n, b) in enumerate(((0, 4, 5), (4, 3, 7))):
                    wait(dve, proj_psum, nth(t, 2, i))
                    js = slice(first, first + n)
                    dve.tensor_tensor(x1[:, js], bank[b][0:PT_, 0:n * C].rearrange("p (j f) -> p j f", j=n),
                                      x_in[:, phase, js], ALU.add).then_inc(x1_ready, 1)
                wait(dve, x1_ready, nth(t, 2, 1))
                norm_stats(1, t, x1, LN_EPS)

            def step(t, phase):
                for g in range(3):
                    add_bias(t, phase, g)
                for g in range(3):
                    find_max(t, g)
                tap(t, phase, 0)
                tap(t, phase, 1)
                values(t, phase, 0)
                tap(t, phase, 2)
                values(t, phase, 1)
                norm_x(t, phase)
                tap(t, phase, 3)
                tap(t, phase, 4)
                for g in range(3):
                    add_up(t, g)
                add_x1(t)
                for i in range(5, 9):
                    tap(t, phase, i)
                add_x(t, phase)

            steps(dve, step)

        @block.gpsimd
        def _(pool):
            pool.memset(bias0, 0.0).then_inc(pool_cleared, 1)
            pool.memset(mh_row, -0.5)
            pool.memset(minus_half[:], -0.5)
            pool.memset(table_load[:], 0.0)
            pool.memset(kbd[:], 0.0)
            pool.memset(prob[:], 0.0)
            pool.memset(xT[:], 0.0)
            pool.memset(qT[:, TOK:], 0.0)
            pool.memset(ymap[:], 0.0).then_inc(pool_cleared, 1)
            pool.wait_ge(pool_cleared, 2)
            pool.wait_ge(dve_set, 8)
            pool.tensor_tensor(std_row, var_eps, mh_row, ALU.pow).then_inc(pool_set, 1)

            def shift(t, g):
                if not has(t):
                    return
                first, n = GROUPS[g]
                wait(pool, max_ready, nth(t, 3, g))
                p = prob[:, HEADS * first:HEADS * (first + n), 0:NT]
                m = smax[:, HEADS * first:HEADS * (first + n)].unsqueeze(2).broadcast_to([128, HEADS * n, NT])
                pool.tensor_tensor(p, p, m, ALU.subtract).then_inc(shifted, 1)

            def divide(t, g):
                if not has(t):
                    return
                first, n = GROUPS[g]
                wait(pool, rec_ready, nth(t, 3, g))
                p = prob[:, HEADS * first:HEADS * (first + n), 0:NT]
                r = srec[:, HEADS * first:HEADS * (first + n)].unsqueeze(2).broadcast_to([128, HEADS * n, NT])
                pool.tensor_tensor(p, p, r, ALU.mult).then_inc(p_ready, 1)

            def root(which, s, dst, src, done):
                b = ln[which]
                wait(pool, ln_ready[which], nth(s, 1, 0))
                pool.tensor_tensor(b["rstd"][:], b["var_eps"][:], minus_half[0:PT_], ALU.pow)\
                    .then_inc(rstd_done[which], 1)
                wait(pool, rstd_done[which], nth(s, 1, 0))
                pool.tensor_tensor(b["offset"][:], b["minus_mean"][:], b["rstd"][:], ALU.mult)\
                    .then_inc(scale_ready[which], 1)
                for j in range(ACT_NORM, WS):
                    last = pool.tensor_scalar(dst[:, j], src[:, j], b["minus_mean"][:, j:j + 1],
                                              b["rstd"][:, j:j + 1], ALU.add, ALU.mult)
                last.then_inc(done, 1)

            def step(t, phase):
                if has(t - 1):
                    wait(pool, x1t_psum, nth(t - 2, 2, 1))
                    root(1, t - 1, x1n, x1, x1n_rest)
                shift(t, 0)
                shift(t, 1)
                shift(t, 2)
                if has(t + 2):
                    wait(pool, xt_psum, nth(t + 1, 2, 1))
                    root(0, t + 2, xn, x_in[:, (phase + 2) % UNROLL], xn_rest)
                for g in range(3):
                    divide(t, g)

            steps(pool, step)


_F = "float32"
_BLOCK = "L0_conv_"
_CONV = "L1_conv_"
_INS = ([_BLOCK + n for n in ("qkv_w", "qkv_b", "proj_w", "proj_b", "rel_bias", "ln1_g", "ln1_b", "ln2_g", "ln2_b",
                              "fc1_w", "fc1_b", "fc2_w", "fc2_b")]
        + [_CONV + n for n in ("dw_kernel", "dw_bias", "pw_kernel", "pw_bias", "gamma", "beta", "moving_mean",
                               "moving_var")])


def constants():
    eye = np.eye(128, dtype=_F)
    rolled = np.zeros((PT_, PT_), _F)
    for r in range(WS):
        for w in range(NWIN):
            rolled[r * NWIN + (w + 1) % NWIN, r * NWIN + w] = 1.0
    col, row = np.arange(NT) // WS, np.arange(NT) % WS
    far_col, far_row = col >= WS - SHIFT, row >= WS - SHIFT
    apart_col = far_col[:, None] != far_col[None, :]
    apart_row = far_row[:, None] != far_row[None, :]
    mask = np.zeros((128, 2, 2, NT), _F)
    for last_strip in range(2):
        for last_pair in range(2):
            for side in range(2):
                apart = (apart_row if last_strip else np.zeros_like(apart_row)) | (
                    apart_col if last_pair and side else np.zeros_like(apart_col))
                mask[64 * side:64 * side + NT, last_strip, last_pair] = np.where(apart, MASKED, 0.0)
    blocks = np.zeros((128, 4, C), _F)
    blocks[0:64, :, 0:HD] = 1.0
    blocks[64:128, :, HD:2 * HD] = 1.0
    blocks[0:64, 0:2, 2 * HD:] = 1.0
    blocks[64:128, 2:4, 2 * HD:] = 1.0
    return {"eye": eye, "rolled_eye": rolled, "mask": mask, "head_blocks": blocks}


def kernel(**inputs):
    import concourse.bacc as bacc
    from concourse.bass_utils import run_bass_kernel_spmd

    nc = bacc.Bacc("TRN2", target_bir_lowering=False, num_devices=1)
    arrays, args = {}, []

    def give(name, a):
        a = np.ascontiguousarray(a)
        arrays[name] = a
        args.append(nc.dram_tensor(name, a.shape, mybir.dt.from_np(a.dtype), kind="ExternalInput").ap())

    give("in_x", inputs["x"])
    for name in _INS:
        a = np.asarray(inputs[name])
        if name.endswith("rel_bias"):
            side = 2 * WS - 1
            a = a.reshape(side, side, HEADS)[::-1, ::-1].transpose(2, 1, 0)
        elif name.endswith("qkv_b"):
            a = a.reshape(3, C).T
        elif name.endswith("fc1_b"):
            a = a.reshape(MC, 128).T
        elif name.endswith("dw_kernel"):
            a = a.reshape(9, C).T
        give("in_" + name, a)
    for name, a in constants().items():
        give("const_" + name, a)
    shape = tuple(inputs["x"].shape)
    args.append(nc.dram_tensor("out_0", shape, F32, kind="ExternalOutput").ap())
    swin_conv_kernel(nc, *args)
    r = run_bass_kernel_spmd(nc, [arrays], core_ids=[0])
    return r.results[0]["out_0"]
```

```python
from contextlib import ExitStack

import numpy as np

import concourse.bass as bass
from concourse import mybir

ALU = mybir.AluOpType
ACT = mybir.ActivationFunctionType
F32 = mybir.dt.float32
AX_X = mybir.AxisListType.X

WS, SHIFT = 7, 3
NT = WS * WS
HW, C, HEADS = 112, 96, 3
HD = C // HEADS
NWIN = HW // WS
TOK = WS * HW
PT_ = WS * NWIN
HALF = TOK // 2
HID = 4 * C
MC = HID // 128
PAIRS = NWIN // 2
PAIR = 64 + NT
GROUPS = [(0, 3), (3, 3), (6, 2)]
HEAD_ORDER = ((0, 1, 2), (2, 0, 1))
HALVES = ((0, 4), (4, 3))
SCALE = float(HD) ** -0.5
LN_EPS, BN_EPS = 1e-4, 1e-3
MASKED = -100.0

MAP_W = HW + 2
AREA = 10
AREAS = 5
TOP_ROWS, LOW_ROWS = 5, 2

ACT_NORM = HALVES[0][1]
LOOP_FIRST = 6
BIAS_LOADS = NT + 1
KEYS = 4 * 16
UNROLL = 4


def swin_conv_kernel(nc, x, qkv_w, qkv_b, proj_w, proj_b, rel_bias_rt, ln1_g, ln1_b, ln2_g, ln2_b,
                     fc1_w, fc1_b, fc2_w, fc2_b, dw_kernel, dw_bias, pw_kernel, pw_bias, gamma, beta,
                     moving_mean, moving_var, eye, rolled_eye, mask, head_blocks, out):
    B = x.shape[0]
    NS = B * NWIN
    LOOPS = (NS - 3 - LOOP_FIRST) // UNROLL

    x_chunks = x.rearrange("b h (c j) f -> (b h c) (j f)", j=WS)
    out_rows = out.rearrange("b h w f -> (b h) w f")

    def nth(strip, tiles, tile):
        if isinstance(strip, int) and strip > NS - 1:
            return tiles * NS
        return tiles * strip + tile + 1

    def wait(eng, sem, count):
        if isinstance(count, int) and count <= 0:
            return
        eng.wait_ge(sem, count)

    def has(strip):
        return not isinstance(strip, int) or 0 <= strip < NS

    def start(value, most):
        if isinstance(value, int):
            return value
        return nc.s_assert_within(value, 0, most,
                                  skip_runtime_bounds_check_because="it follows from the strip's number")

    def steps(eng, step, first=-2):
        for t in range(first, LOOP_FIRST):
            step(t, t % UNROLL)
        with eng.Fori(0, LOOPS) as it:
            for u in range(UNROLL):
                step(it * UNROLL + (LOOP_FIRST + u), (LOOP_FIRST + u) % UNROLL)
        for t in range(LOOP_FIRST + UNROLL * LOOPS, NS + 4):
            step(t, t % UNROLL)

    def is_zero(value, period):
        return 1 - (value + period - 1) // period

    def area_of_strip(s):
        k = s % NWIN
        own = k % 2 + (k + 1) // NWIN + is_zero(s % (2 * NWIN), 2 * NWIN) * 3 \
            + is_zero((s + NWIN) % (2 * NWIN), 2 * NWIN) * 4
        return own * AREA

    def area_below_strip(s):
        k = (s + 1) % NWIN
        below = k % 2 + (k + 1) // NWIN + is_zero((s + 1) % (2 * NWIN), 2 * NWIN) * 4 \
            + is_zero((s + 1 + NWIN) % (2 * NWIN), 2 * NWIN) * 3
        return below * AREA

    with ExitStack() as ctx:
        def sb(name, *shape):
            return ctx.enter_context(nc.sbuf_tensor(name, list(shape), F32))

        def sem(name):
            return ctx.enter_context(nc.semaphore(name))

        ident = sb("ident", 128, 128)
        roll = sb("roll", PT_, PT_)
        heads = sb("heads", 128, 4, C)
        table = sb("table", 128, 2, PAIRS * HEADS, NT)
        wqkv = sb("wqkv", C, 2 * C + 4 * HD)
        wproj = sb("wproj", C + 1, C)
        w1 = sb("w1", C, HID)
        w2 = sb("w2", 128, MC, C)
        wpw = sb("wpw", C + 1, C)
        taps = sb("taps", C, 9)
        cols = sb("cols", C, 8)
        bqkv = sb("bqkv", C, 3)
        bfc1 = sb("bfc1", 128, MC)
        minus_half = sb("minus_half", 128, WS)
        table_load = sb("table_load", 1, 2)

        x_in = sb("x_in", PT_, 4, WS, C)
        xn = sb("xn", PT_, WS, C)
        x1 = sb("x1", PT_, WS, C)
        x1n = sb("x1n", PT_, WS, C)
        o_tile = sb("o_tile", HW, 2, WS, C)
        xT = sb("xT", C, TOK)
        qT = sb("qT", C, TOK)
        kT = sb("kT", C, TOK)
        kbd = sb("kbd", C, HEADS + 1, TOK)
        prob = sb("prob", 128, PAIRS * HEADS, 64)
        vbd = sb("vbd", 128, 2, NWIN * C)
        probT = sb("probT", PAIR, 4, 3, PAIR)
        attnT = sb("attnT", C + 1, NT, NWIN)
        x1T = sb("x1T", C, TOK)
        hT = sb("hT", 128, MC, TOK)
        acc = sb("acc", C + 1, 2, WS, HW)
        ymap = sb("ymap", C, AREAS * AREA, MAP_W)
        smax = sb("smax", 128, PAIRS * HEADS)
        ssum = sb("ssum", 128, PAIRS * HEADS)
        srec = sb("srec", 128, PAIRS * HEADS)
        ln = [{name: sb(f"{name}{i}", PT_, *shape) for name, shape in
               (("stats", (WS, 6)), ("sum", (WS,)), ("diff", (WS,)), ("dev", (WS,)), ("between", (WS,)),
                ("within", (WS,)), ("minus_mean", (WS,)), ("var_eps", (WS,)), ("rstd", (WS,)),
                ("offset", (WS,)))} for i in (1, 2)]

        bank = [ctx.enter_context(nc.psum_tensor(f"bank{i}", [128, 512], F32)) for i in range(8)]

        const_loaded, rows_loaded = sem("const_loaded"), sem("rows_loaded")
        bias_loaded, row_moved = sem("bias_loaded"), sem("row_moved")
        pool_cleared, dve_set, pe_set, pool_set = sem("pool_cleared"), sem("dve_set"), sem("pe_set"), sem("pool_set")
        dve_cleared, row_step = sem("dve_cleared"), sem("row_step")
        x_loaded = [sem(f"x_loaded{i}") for i in range(4)]
        out_stored = [sem(f"out_stored{i}") for i in range(2)]
        k_ready = sem("k_ready")
        xt_psum, q_psum, k_psum, v_psum = sem("xt_psum"), sem("q_psum"), sem("k_psum"), sem("v_psum")
        s_psum, pt_psum, o_psum, proj_psum = sem("s_psum"), sem("pt_psum"), sem("o_psum"), sem("proj_psum")
        x1t_psum, h_psum, y_psum, yt_psum = sem("x1t_psum"), sem("h_psum"), sem("y_psum"), sem("yt_psum")
        pw_psum = sem("pw_psum")
        xt_ready, q_ready, k_copied, exp_done = sem("xt_ready"), sem("q_ready"), sem("k_copied"), sem("exp_done")
        pt_ready, o_ready, x1t_ready = sem("pt_ready"), sem("o_ready"), sem("x1t_ready")
        h_ready, ymap_ready, out_ready = sem("h_ready"), sem("ymap_ready"), sem("out_ready")
        xn_ready, x1n_ready = sem("xn_ready"), sem("x1n_ready")
        s_biased, max_ready, sum_done, rec_ready = sem("s_biased"), sem("max_ready"), sem("sum_done"), sem("rec_ready")
        v_ready, y_ready, x1_ready = sem("v_ready"), sem("y_ready"), sem("x1_ready")
        stats_done = [sem("stats1_done"), sem("stats2_done")]
        parts_done = [sem("parts1_done"), sem("parts2_done")]
        halves_done = [sem("halves1_done"), sem("halves2_done")]
        ln_ready = [sem("ln1_ready"), sem("ln2_ready")]
        top_done, low_done = sem("top_done"), sem("low_done")
        shifted, p_ready = sem("shifted"), sem("p_ready")
        rstd_done = [sem("rstd1_done"), sem("rstd2_done")]
        scale_ready = [sem("scale1_ready"), sem("scale2_ready")]
        xn_rest, x1n_rest = sem("xn_rest"), sem("x1n_rest")

        bias0 = hT[:, 0, 0:HEADS * NT]
        maskt = hT[:, 1, 0:4 * NT].rearrange("p (a b m) -> p a b m", a=2, b=2)
        pw_raw = hT[0:C, 2, 0:C]
        qkv_raw = hT[0:C, 2, C:4 * C]
        proj_row = hT[0:1, 2, 4 * C:5 * C]
        w1_raw = x1T[:, 0:HID]
        rows = x1[0:1].rearrange("p j f -> p (j f)")
        proj_b_row, pw_b_row, beta_row, mean_row = (
            rows[:, i * C:(i + 1) * C] for i in range(4))
        scratch = x1n[0:1].rearrange("p j f -> p (j f)")
        row_a, row_b, pw_row = (scratch[:, i * C:(i + 1) * C] for i in range(3))
        ones, bn_diag = xn[0:C, 0], xn[0:C, 1]
        var_eps, inv_std, bn_factor = (xn[0:C, 2, i:i + 1] for i in range(3))

        block = ctx.enter_context(nc.Block())

        @block.sync
        def _(sp):
            const = [
                (ident[:], eye), (roll[:], rolled_eye), (heads[:], head_blocks), (maskt, mask),
                (qkv_raw, qkv_w), (wproj[0:C], proj_w), (w1_raw, fc1_w),
                (w2[:], fc2_w.rearrange("(m p) n -> p m n", p=128)),
                (pw_raw, pw_kernel.rearrange("a b i o -> (a b i) o")),
                (taps[:], dw_kernel),
                (bqkv[:], qkv_b),
                (bfc1[:], fc1_b),
            ] + [(cols[:, i:i + 1], v.rearrange("(f u) -> f u", u=1))
                 for i, v in enumerate((ln1_g, ln1_b, ln2_g, ln2_b, fc2_b, dw_bias, gamma, moving_var))]
            for dst, src in const:
                sp.dma_start(dst, src).then_inc(const_loaded, 16)
            for dst, src in ((proj_b_row, proj_b), (pw_b_row, pw_bias), (beta_row, beta),
                             (mean_row, moving_mean)):
                sp.dma_start(dst, src.rearrange("(u f) -> u f", u=1)).then_inc(rows_loaded, 16)

            def load(t, phase):
                s = t + 3
                if not has(s):
                    return
                slot = (phase + 3) % UNROLL
                wait(sp, x1_ready, nth(t - 1, 2, 1))
                image, k = s // NWIN, s % NWIN
                first = (image * HW + k * WS + SHIFT) * NWIN
                wrapped = (image * HW + (k + 1) % NWIN * WS) * NWIN
                top = (WS - SHIFT) * NWIN
                dst = x_in[:, slot].rearrange("p j f -> p (j f)")
                sp.dma_start(dst[0:top], x_chunks[bass.ds(start(first, B * HW * NWIN - top), top)]).then_inc(x_loaded[slot], 16)
                sp.dma_start(dst[top:PT_], x_chunks[bass.ds(start(wrapped, B * HW * NWIN - (PT_ - top)), PT_ - top)]).then_inc(x_loaded[slot], 16)

            def spread_keys(t):
                if not has(t + 1):
                    return
                wait(sp, s_psum, nth(t, 3, 2))
                wait(sp, k_copied, nth(t + 1, 2, 1))
                for h, part in ((0, 1), (1, 2), (2, 0), (2, 3)):
                    hp = slice(h * HD, (h + 1) * HD)
                    sp.dma_start(kbd[hp, part, :], kT[hp, :]).then_inc(k_ready, 16)

            def store(t, phase):
                i = t - 4
                if not has(i):
                    return
                slot = phase % 2
                wait(sp, out_ready, nth(i, 2, 1))
                image, k = i // NWIN, (i + 1) % NWIN
                top = image * HW + k * WS + 2
                low = image * HW + (k + 1) % NWIN * WS
                for row, at, n in ((top, 0, TOP_ROWS), (low, TOP_ROWS, LOW_ROWS)):
                    sp.dma_start(out_rows[bass.ds(start(row, B * HW - n), n)].rearrange("r w f -> w r f"),
                                 o_tile[:, slot, at:at + n]).then_inc(out_stored[slot], 16)

            def step(t, phase):
                load(t, phase)
                spread_keys(t)
                store(t, phase)

            load(-3, 1)
            load(-2, 2)
            sp.wait_ge(dve_set, 6)
            sp.dma_start(wproj[C:C + 1], proj_row).then_inc(row_moved, 16)
            sp.wait_ge(dve_set, 11)
            sp.dma_start(wpw[C:C + 1], pw_row).then_inc(row_moved, 16)
            sp.wait_ge(pool_cleared, 1)
            side = 2 * WS - 1
            for jx in range(WS):
                for ry in range(WS):
                    n = jx * WS + ry
                    src = rel_bias_rt[:, WS - 1 - jx:side - jx, WS - 1 - ry:side - ry]
                    sp.dma_start(bias0[n:n + 1], src).then_inc(bias_loaded, 16)
            sp.wait_ge(bias_loaded, 16 * NT)
            sp.dma_start(bias0[64:64 + NT], bias0[0:NT]).then_inc(bias_loaded, 16)

            sp.wait_ge(dve_cleared, 2)
            steps(sp, step, first=-1)
            stores = [(NS + 1) // 2, NS // 2]
            sp.wait_ge(out_stored[1], 32 * stores[0])
            sp.wait_ge(out_stored[0], 32 * stores[1])

        @block.tensor
        def _(pe):
            pe.wait_ge(dve_cleared, 1)
            pe.wait_ge(const_loaded, 16 * 20)
            pe.wait_ge(rows_loaded, 16 * 4)
            for i in range(3):
                pe.matmul(bank[0][0:C, i:i + 1], qkv_raw[:, i * C:(i + 1) * C], cols[:, 1:2], start=True, stop=True)
            for m in range(MC):
                pe.matmul(bank[1][:, m:m + 1], w1_raw[:, m * 128:(m + 1) * 128], cols[:, 3:4], start=True, stop=True)
            pe.matmul(bank[2][0:1, 0:C], cols[:, 5:6], pw_raw, start=True, stop=True).then_inc(pe_set, 1)
            pe.wait_ge(dve_set, 3)
            pe.matmul(bank[3][0:1, 0:C], bqkv[:, 2:3], wproj[0:C], start=True, stop=True).then_inc(pe_set, 1)
            pe.wait_ge(dve_set, 10)
            pe.matmul(bank[4][0:C, 0:C], ones, bn_diag, start=True, stop=True).then_inc(pe_set, 1)
            pe.wait_ge(dve_set, 12)
            pe.wait_ge(row_moved, 32)
            pe.wait_ge(pool_cleared, 2)
            pe.wait_ge(dve_cleared, 2)

            def scores(t):
                if not has(t):
                    return
                wait(pe, q_ready, nth(t, 2, 1))
                wait(pe, k_ready, KEYS * nth(t, 1, 0))
                for g, (first, n) in enumerate(GROUPS):
                    if g == 0:
                        wait(pe, xt_ready, nth(t + 1, 2, 1))
                    elif g == 1:
                        wait(pe, y_ready, nth(t - 2, 2, 1))
                    else:
                        wait(pe, ymap_ready, nth(t - 2, 2, 1))
                    for p in range(n):
                        for side in range(2):
                            w = 2 * (first + p) + side
                            mm = pe.matmul(bank[g][64 * side:64 * side + NT, p * HEADS * NT:(p + 1) * HEADS * NT],
                                           qT[:, w * NT:(w + 1) * NT],
                                           kbd[:, 1 - (first + p) % 2:4 - (first + p) % 2, w * NT:(w + 1) * NT],
                                           start=True, stop=True)
                    mm.then_inc(s_psum, 1)

            def queries_keys(t):
                if not has(t + 1):
                    return
                wait(pe, xt_ready, nth(t + 1, 2, 1))
                for u in range(2):
                    if u == 0:
                        wait(pe, pt_ready, nth(t - 1, 4, 1))
                    else:
                        wait(pe, ymap_ready, nth(t - 2, 2, 0))
                    pe.matmul(bank[3 + u][0:C, 0:HALF], wqkv[:, 0:C], xT[:, u * HALF:(u + 1) * HALF],
                              start=True, stop=True).then_inc(q_psum, 1)
                for u in range(2):
                    if u == 0:
                        wait(pe, x1_ready, nth(t - 1, 2, 0))
                    else:
                        wait(pe, o_ready, nth(t - 1, 3, 1))
                    pe.matmul(bank[5 + u][0:C, 0:HALF], wqkv[:, C:2 * C], xT[:, u * HALF:(u + 1) * HALF],
                              start=True, stop=True).then_inc(k_psum, 1)

            def values(t, tiles):
                if not has(t + 1):
                    return
                for i in tiles:
                    wait(pe, s_biased, nth(t, 3, i + 1))
                    for j in range(8):
                        for side in range(2):
                            rhs = wqkv[:, 2 * C + side * 2 * HD:2 * C + (side + 1) * 2 * HD]
                            mm = pe.matmul(bank[1 + i][64 * side:64 * side + NT, j * 2 * HD:(j + 1) * 2 * HD],
                                           xT[:, (8 * i + j) * NT:(8 * i + j + 1) * NT], rhs, start=True, stop=True)
                    mm.then_inc(v_psum, 1)

            def turn_x1(t):
                if not has(t - 1):
                    return
                for i, (js, b) in enumerate(((range(4, 7), 0), (range(0, 4), 7))):
                    if i == 0:
                        wait(pe, x1n_rest, nth(t - 1, 1, 0))
                        wait(pe, s_biased, nth(t, 3, 0))
                    else:
                        wait(pe, x1n_ready, nth(t - 1, 1, 0))
                        wait(pe, x1_ready, nth(t - 1, 2, 1))
                    for a, j in enumerate(js):
                        mm = pe.transpose(bank[b][0:C, a * PT_:(a + 1) * PT_], x1n[:, j, :], ident[0:PT_, 0:PT_])
                    mm.then_inc(x1t_psum, 1)

            def hidden(t, half):
                if not has(t - 1):
                    return
                for i in range(MC * half, MC * (half + 1)):
                    m = i % MC
                    first, n = ((0, 4), (4, 3))[half]
                    if m == 0:
                        wait(pe, x1t_ready, nth(t - 1, 2, 1 - half))
                    if i < 2:
                        wait(pe, k_copied, nth(t + 1, 2, i))
                    elif i == 2:
                        wait(pe, x1t_ready, nth(t - 1, 2, 1))
                    else:
                        wait(pe, h_ready, nth(t - 1, 6, i - 3))
                    pe.matmul(bank[5 + i % 3][:, 0:n * PT_], w1[:, m * 128:(m + 1) * 128],
                              x1T[:, first * PT_:(first + n) * PT_], start=True, stop=True).then_inc(h_psum, 1)

            def second_layer(t):
                if not has(t - 1):
                    return
                for half, (first, n) in enumerate(((0, 4), (4, 3))):
                    wait(pe, h_ready, nth(t - 1, 6, 3 * half + 2))
                    if half == 0:
                        wait(pe, x1t_ready, nth(t - 1, 2, 0))
                    else:
                        wait(pe, v_ready, nth(t + 1, 2, 0))
                        wait(pe, s_biased, nth(t, 3, 1))
                    for a in range(n):
                        j = first + a
                        for m in range(MC):
                            mm = pe.matmul(bank[half][0:PT_, a * C:(a + 1) * C], hT[:, m, j * PT_:(j + 1) * PT_],
                                           w2[:, m, :], start=(m == 0), stop=(m == MC - 1))
                    mm.then_inc(y_psum, 1)

            prob_flat = prob[0:PAIR].rearrange("p a m -> p (a m)")

            def turn_probs(t, d):
                wait(pe, p_ready, nth(t, 3, (2 * d + 1) // 3))
                if d == 0:
                    wait(pe, v_ready, nth(t + 1, 2, 1))
                elif d < 3:
                    wait(pe, q_ready, nth(t + 1, 2, d - 1))
                    wait(pe, out_ready, nth(t - 4, 2, d - 1))
                else:
                    wait(pe, pt_ready, nth(t, 4, 0))
                b = bank[(2, 3, 4, 2)[d]]
                for i, slot in enumerate((0, 4, 2)):
                    mm = pe.transpose(b[0:PAIR, i * PAIR:(i + 1) * PAIR], prob_flat[:, (6 * d + slot) * 64:][:, 0:PAIR],
                                      ident[0:PAIR, 0:PAIR])
                mm.then_inc(pt_psum, 1)

            def weigh_values(t, phase, d):
                if d == 0:
                    wait(pe, v_ready, nth(t, 2, 1))
                    wait(pe, h_ready, nth(t - 1, 6, 3))
                if d == 2:
                    wait(pe, h_ready, nth(t - 1, 6, 4))
                wait(pe, pt_ready, nth(t, 4, d))
                if d == 3:
                    wait(pe, xt_ready, nth(t + 2, 2, 0))
                b, v = bank[(5, 5, 6, 7)[d]], vbd[:, phase % 2]
                for j in range(4):
                    w = 4 * d + j
                    at = (w % 8) * NT
                    side = 64 * (j % 2)
                    for h in range(HEADS):
                        mm = pe.matmul(b[h * HD:(h + 1) * HD, at:at + NT], v[0:PAIR, w * C + h * HD:w * C + (h + 1) * HD],
                                       probT[:, d, j // 2 if h < 2 else 2, side:side + NT], start=True, stop=True)
                if d > 0:
                    mm.then_inc(o_psum, 1)

            def turn_x(t, i):
                if not has(t + 2):
                    return
                wait(pe, xn_ready, nth(t + 2, 1, 0))
                wait(pe, xn_rest, nth(t + 2, 1, 0))
                js, perm, b = ((range(3, 7), ident[0:PT_, 0:PT_], 7), (range(0, 3), roll[:], 0))[i]
                if i == 0:
                    wait(pe, h_ready, nth(t - 1, 6, 5))
                else:
                    wait(pe, y_ready, nth(t - 1, 2, 0))
                for a, j in enumerate(js):
                    mm = pe.transpose(bank[b][0:C, a * PT_:(a + 1) * PT_], xn[:, j, :], perm)
                mm.then_inc(xt_psum, 1)

            def pointwise(t, phase):
                if not has(t - 4):
                    return
                wait(pe, top_done, nth(t - 4, 9, 8))
                wait(pe, low_done, nth(t - 4, 9, 8))
                for i, ((first, n), b) in enumerate(zip(HALVES, (3, 4))):
                    wait(pe, q_ready, nth(t + 1, 2, i))
                    wait(pe, ymap_ready, nth(t - 2, 2, 1))
                    wait(pe, out_ready, nth(t - 5, 2, i))
                    for a in range(n):
                        mm = pe.matmul(bank[b][0:HW, a * C:(a + 1) * C], acc[:, phase % 2, first + a, :], wpw[:],
                                       start=True, stop=True)
                    mm.then_inc(pw_psum, 1)

            def turn_y(t):
                if not has(t - 1):
                    return
                for i, (first, n, b) in enumerate(((0, 4, 4), (4, 3, 2))):
                    wait(pe, y_ready, nth(t - 1, 2, i))
                    wait(pe, pt_ready, nth(t, 4, i + 2))
                    if i == 0:
                        wait(pe, out_ready, nth(t - 4, 2, 1))
                    for a in range(n):
                        mm = pe.transpose(bank[b][0:C, a * PT_:(a + 1) * PT_], x1[:, first + a, :],
                                          ident[0:PT_, 0:PT_])
                    mm.then_inc(yt_psum, 1)

            def project(t):
                if not has(t):
                    return
                wait(pe, o_ready, nth(t, 3, 2))
                for i, (first, n, b) in enumerate(((0, 4, 5), (4, 3, 7))):
                    if i == 1:
                        wait(pe, xt_ready, nth(t + 2, 2, 0))
                    for a in range(n):
                        j = first + a
                        col = j - SHIFT if j >= SHIFT else j - SHIFT + WS
                        mm = pe.matmul(bank[b][0:PT_, a * C:(a + 1) * C],
                                       attnT[:, col * WS:(col + 1) * WS, :], wproj[:],
                                       start=True, stop=True)
                    mm.then_inc(proj_psum, 1)

            def step(t, phase):
                scores(t)
                queries_keys(t)
                values(t, (0,))
                turn_x1(t)
                values(t, (1,))
                hidden(t, 0)
                hidden(t, 1)
                pointwise(t, phase)
                second_layer(t)
                turn_x(t, 0)
                if has(t):
                    for d in range(3):
                        turn_probs(t, d)
                turn_x(t, 1)
                if has(t):
                    weigh_values(t, phase, 0)
                    turn_probs(t, 3)
                    for d in range(1, 4):
                        weigh_values(t, phase, d)
                turn_y(t)
                project(t)

            steps(pe, step)

        @block.scalar
        def _(act):
            act.wait_ge(dve_set, 12)
            act.wait_ge(pool_cleared, 2)
            act.wait_ge(dve_cleared, 2)

            def exps(t, g):
                if not has(t):
                    return
                first, n = GROUPS[g]
                wait(act, shifted, nth(t, 3, g))
                p = prob[:, HEADS * first:HEADS * (first + n), 0:NT]
                act.activation(p, p, ACT.Exp).then_inc(exp_done, 1)

            def queries(t):
                if not has(t + 1):
                    return
                wait(act, s_psum, nth(t, 3, 2))
                for u in range(2):
                    wait(act, q_psum, nth(t + 1, 2, u))
                    act.activation(qT[:, u * HALF:(u + 1) * HALF], bank[3 + u][0:C, 0:HALF], ACT.Identity,
                                   bias=bqkv[:, 0:1], scale=SCALE).then_inc(q_ready, 1)

            def keys(t, u):
                if not has(t + 1):
                    return
                if u == 0:
                    wait(act, k_ready, KEYS * nth(t, 1, 0))
                wait(act, k_psum, nth(t + 1, 2, u))
                act.activation(kT[:, u * HALF:(u + 1) * HALF], bank[5 + u][0:C, 0:HALF], ACT.Identity,
                               bias=bqkv[:, 1:2]).then_inc(k_copied, 1)

            def outputs(t, phase):
                if not has(t - 4):
                    return
                slot = phase % 2
                wait(act, out_stored[slot], 32 * ((t - 4) // 2))
                for i, ((first, n), b) in enumerate(zip(HALVES, (3, 4))):
                    wait(act, pw_psum, nth(t - 4, 2, i))
                    act.copy(o_tile[:, slot, first:first + n],
                             bank[b][0:HW, 0:n * C].rearrange("p (r f) -> p r f", r=n)).then_inc(out_ready, 1)

            def normalise(which, s, dst, src, ready):
                b = ln[which]
                wait(act, scale_ready[which], nth(s, 1, 0))
                for j in range(ACT_NORM):
                    last = act.activation(dst[:, j], src[:, j], ACT.Identity, bias=b["offset"][:, j:j + 1],
                                          scale=b["rstd"][:, j:j + 1])
                last.then_inc(ready, 1)

            def x1_turned(t):
                if not has(t - 1):
                    return
                wait(act, h_psum, nth(t - 2, 6, 5))
                for i, (first, n, b) in enumerate(((4, 3, 0), (0, 4, 7))):
                    wait(act, x1t_psum, nth(t - 1, 2, i))
                    act.copy(x1T[:, first * PT_:(first + n) * PT_], bank[b][0:C, 0:n * PT_]).then_inc(x1t_ready, 1)

            def gelus(t):
                if not has(t - 1):
                    return
                act.activation(table_load[:, 1:2], table_load[:, 0:1], ACT.Gelu_apprx_tanh)
                wait(act, y_psum, nth(t - 2, 2, 1))
                for i in range(2 * MC):
                    half, m = i // MC, i % MC
                    first, n = ((0, 4), (4, 3))[half]
                    wait(act, h_psum, nth(t - 1, 6, i))
                    act.activation(hT[:, m, first * PT_:(first + n) * PT_], bank[5 + i % 3][:, 0:n * PT_],
                                   ACT.Gelu_apprx_tanh, bias=bfc1[:, m:m + 1]).then_inc(h_ready, 1)

            def probs_turned(t, tiles):
                if not has(t):
                    return
                wait(act, o_psum, nth(t - 1, 3, 2))
                for d in tiles:
                    wait(act, pt_psum, nth(t, 4, d))
                    act.copy(probT[:, d].rearrange("p i n -> p (i n)"), bank[(2, 3, 4, 2)[d]][0:PAIR, 0:3 * PAIR])\
                        .then_inc(pt_ready, 1)

            def attention_out(t):
                if not has(t):
                    return
                wait(act, proj_psum, nth(t - 1, 2, 1))
                far = (WS - SHIFT) * WS
                dst = attnT[0:C].rearrange("p n w -> p w n")
                for u, (first, n, b) in enumerate(((0, 8, 5), (8, 4, 6), (12, 4, 7))):
                    wait(act, o_psum, nth(t, 3, u))
                    at = (first % 8) * NT
                    src = bank[b][0:C, at:at + n * NT].rearrange("p (w n) -> p w n", w=n)
                    act.copy(dst[:, first:first + n, 0:far], src[:, :, 0:far])
                    inner = min(n, NWIN - 1 - first)
                    last = act.copy(dst[:, first + 1:first + 1 + inner, far:], src[:, 0:inner, far:])
                    if inner < n:
                        last = act.copy(dst[:, 0, far:], src[:, inner, far:])
                    last.then_inc(o_ready, 1)

            def x_turned(t, i):
                if not has(t + 2):
                    return
                first, n, b = ((0, 4, 7), (4, 3, 0))[i]
                wait(act, v_psum, nth(t + 1, 2, 1))
                wait(act, xt_psum, nth(t + 2, 2, i))
                src = bank[b][0:C, 0:n * PT_].rearrange("p (n w) -> p n w", w=NWIN)
                dst = xT[:].rearrange("p (w n) -> p n w", w=NWIN)[:, first * WS:(first + n) * WS, :]
                act.copy(dst, src).then_inc(xt_ready, 1)

            def into_map(t, phase):
                if not has(t - 1):
                    return
                s = t - 1
                wait(act, top_done, nth(t - 3, 9, 8))
                wait(act, low_done, nth(t - 3, 9, 8))
                area = area_of_strip(s)
                if phase == 0:
                    parts = [(0, 4, area + 2), (4, 3, area + 6 + (s % NWIN + 1) // NWIN)]
                else:
                    parts = [(0, 7, area + 2)]
                parts.append((5, 2, area_below_strip(s)))
                for i, ((first, n), b) in enumerate(zip(HALVES, (4, 2))):
                    wait(act, yt_psum, nth(s, 2, i))
                    src = bank[b][0:C, 0:n * PT_].rearrange("p (j r c) -> p j r c", j=n, r=WS)
                    for r0, nr, row in parts:
                        dst = ymap[:, bass.ds(start(row, AREAS * AREA - nr), nr), 1:1 + HW].rearrange("p r (c j) -> p j r c", j=WS)
                        last = act.activation(dst[:, first:first + n], src[:, :, r0:r0 + nr, :], ACT.Relu,
                                              bias=cols[:, 4:5])
                    last.then_inc(ymap_ready, 1)

            def step(t, phase):
                queries(t)
                if has(t - 1):
                    wait(act, x1t_psum, nth(t - 2, 2, 1))
                    normalise(1, t - 1, x1n, x1, x1n_ready)
                keys(t, 0)
                x1_turned(t)
                keys(t, 1)
                gelus(t)
                for g in range(3):
                    exps(t, g)
                if has(t + 2):
                    wait(act, xt_psum, nth(t + 1, 2, 1))
                    normalise(0, t + 2, xn, x_in[:, (phase + 2) % UNROLL], xn_ready)
                outputs(t, phase)
                probs_turned(t, range(0, 3))
                x_turned(t, 0)
                probs_turned(t, range(3, 4))
                x_turned(t, 1)
                attention_out(t)
                into_map(t, phase)

            steps(act, step)

        @block.vector
        def _(dve):
            dve.memset(attnT[C:C + 1], 1.0)
            dve.memset(acc[C:C + 1], 1.0)
            dve.memset(ones, 1.0).then_inc(dve_set, 1)
            for b in range(3):
                last = dve.memset(bank[b][:], 0.0)
            last.then_inc(dve_cleared, 1)
            dve.memset(kbd[:], 0.0)
            dve.memset(ymap[:], 0.0).then_inc(dve_cleared, 1)
            dve.wait_ge(const_loaded, 16 * 20)
            dve.wait_ge(rows_loaded, 16 * 4)
            dve.wait_ge(pe_set, 1)
            dve.tensor_tensor(bfc1[:], bank[1][:, 0:MC], bfc1[:], ALU.add).then_inc(dve_set, 1)
            dve.tensor_tensor(bqkv[:], bank[0][0:C, 0:3], bqkv[:], ALU.add).then_inc(dve_set, 1)
            dve.wait_ge(dve_set, 3)
            dve.tensor_scalar(bqkv[:, 0:1], bqkv[:, 0:1], SCALE, None, ALU.mult).then_inc(dve_set, 1)
            dve.tensor_scalar(wqkv[:, 0:2 * C], qkv_raw[:, 0:2 * C], cols[:, 0:1], None, ALU.mult)
            raw_heads = qkv_raw[:, 2 * C:3 * C].rearrange("p (h f) -> p h f", h=HEADS)
            v_heads = wqkv[:, 2 * C:].rearrange("p (h f) -> p h f", h=4)
            dve.tensor_scalar(v_heads[:, 0:2], raw_heads[:, 0:3:2], cols[:, 0:1], None, ALU.mult)
            dve.tensor_scalar(v_heads[:, 2:4], raw_heads[:, 1:3], cols[:, 0:1], None, ALU.mult)\
                .then_inc(dve_set, 1)
            dve.wait_ge(pe_set, 2)
            dve.tensor_tensor(proj_row, bank[3][0:1, 0:C], proj_b_row, ALU.add).then_inc(dve_set, 1)
            dve.tensor_scalar(w1[:], w1_raw, cols[:, 2:3], None, ALU.mult).then_inc(dve_set, 1)
            dve.tensor_scalar(var_eps, cols[:, 7:8], BN_EPS, None, ALU.add).then_inc(dve_set, 1)
            dve.wait_ge(pool_set, 1)
            dve.tensor_tensor(bn_factor, inv_std, cols[:, 6:7], ALU.mult).then_inc(dve_set, 1)
            dve.wait_ge(dve_set, 9)
            dve.tensor_scalar(bn_diag, ident[0:C, 0:C], bn_factor, None, ALU.mult).then_inc(dve_set, 1)
            dve.tensor_tensor(row_a, bank[2][0:1, 0:C], pw_b_row, ALU.add).then_inc(row_step, 1)
            dve.wait_ge(row_step, 1)
            dve.tensor_tensor(row_b, row_a, mean_row, ALU.subtract).then_inc(row_step, 1)
            dve.wait_ge(row_step, 2)
            dve.wait_ge(pe_set, 3)
            dve.tensor_tensor(row_a, row_b, bank[4][0:1, 0:C], ALU.mult).then_inc(row_step, 1)
            dve.wait_ge(row_step, 3)
            dve.tensor_tensor(pw_row, row_a, beta_row, ALU.add).then_inc(dve_set, 1)
            dve.tensor_tensor(wpw[0:C], bank[4][0:C, 0:C], pw_raw, ALU.mult).then_inc(dve_set, 1)
            dve.wait_ge(dve_set, 12)
            dve.wait_ge(dve_cleared, 2)
            dve.wait_ge(pool_cleared, 2)
            dve.wait_ge(row_moved, 32)

            def build_table():
                dve.wait_ge(bias_loaded, 16 * BIAS_LOADS)
                slots = table[:].rearrange("p l (q h) m -> p l q h m", h=HEADS)
                for last_strip in range(2):
                    for pairs, last_pair in ((range(0, PAIRS, 2), 0), (range(1, PAIRS - 2, 2), 0),
                                             (range(PAIRS - 1, PAIRS), 1)):
                        n = len(pairs)
                        m = maskt[:, last_strip, last_pair].unsqueeze(1).broadcast_to([128, n, NT])
                        for i, h in enumerate(HEAD_ORDER[pairs[0] % 2]):
                            b = bias0[:, h * NT:(h + 1) * NT].unsqueeze(1).broadcast_to([128, n, NT])
                            last = dve.tensor_tensor(slots[:, last_strip, pairs[0]:pairs[-1] + 1:2, i], b, m, ALU.add)
                last.then_inc(dve_set, 1)
                dve.wait_ge(dve_set, 13)

            def add_bias(t, phase, g):
                if not has(t):
                    return
                first, n = GROUPS[g]
                if g == 0:
                    wait(dve, pt_psum, nth(t - 1, 4, 3))
                wait(dve, s_psum, nth(t, 3, g))
                which = (t % NWIN + 1) // NWIN if phase == UNROLL - 1 else 0
                bias = (table[:, which] if isinstance(which, int) else table[:, bass.ds(start(which, 1), 1)].squeeze(1))
                dst = prob[:, HEADS * first:HEADS * (first + n), 0:NT]
                dve.tensor_tensor(dst,
                                  bank[g][:, 0:n * HEADS * NT].rearrange("p (a m) -> p a m", m=NT),
                                  bias[:, HEADS * first:HEADS * (first + n)],
                                  ALU.add).then_inc(s_biased, 1)

            def find_max(t, g):
                if not has(t):
                    return
                first, n = GROUPS[g]
                at = slice(HEADS * first, HEADS * (first + n))
                wait(dve, s_biased, nth(t, 3, g))
                dve.tensor_reduce(smax[:, at], prob[:, at, 0:NT], AX_X, ALU.max).then_inc(max_ready, 1)

            def add_up(t, g):
                if not has(t):
                    return
                first, n = GROUPS[g]
                at = slice(HEADS * first, HEADS * (first + n))
                wait(dve, exp_done, nth(t, 3, g))
                p = prob[:, HEADS * first:HEADS * (first + n), 0:NT]
                dve.tensor_reduce(ssum[:, at], p, AX_X, ALU.add).then_inc(sum_done, 1)
                wait(dve, sum_done, nth(t, 3, g))
                dve.reciprocal(srec[:, at], ssum[:, at]).then_inc(rec_ready, 1)

            def tap(t, phase, i):
                c = t - 3
                if not has(c):
                    return
                dy, dx = i // 3 - 1, i % 3
                top = area_below_strip(c) + 1 + dy
                low = top + TOP_ROWS + ((c + 1) % NWIN + 1) // NWIN
                if i == 0:
                    wait(dve, ymap_ready, nth(c + 1, 2, 1))
                    wait(dve, pw_psum, nth(t - 5, 2, 1))
                for row, at, n, done in ((top, 0, TOP_ROWS, top_done), (low, TOP_ROWS, LOW_ROWS, low_done)):
                    src = ymap[:, bass.ds(start(row, AREAS * AREA - n), n), dx:dx + HW]
                    dst = acc[0:C, (phase + 1) % 2, at:at + n, :]
                    if i == 0:
                        dve.tensor_scalar(dst, src, taps[:, 0:1], None, ALU.mult).then_inc(done, 1)
                    else:
                        wait(dve, done, nth(c, 9, i - 1))
                        dve.scalar_tensor_tensor(out=dst, in0=src, scalar=taps[:, i:i + 1], in1=dst,
                                                 op0=ALU.mult, op1=ALU.add).then_inc(done, 1)

            def values(t, phase, i):
                if not has(t + 1):
                    return
                wait(dve, o_psum, nth(t - 1, 3, 2))
                wait(dve, v_psum, nth(t + 1, 2, i))
                src = bank[1 + i][:].rearrange("p (g w h f) -> p g w h f", g=2, w=4, h=2)
                dst = vbd[:, (phase + 1) % 2, 8 * i * C:8 * (i + 1) * C].rearrange(
                    "p (g w h f) -> p g w h f", g=2, w=4, h=HEADS)
                dve.tensor_tensor(dst[:, :, :, 0:2].rearrange("p g w h f -> p (g w) h f"),
                                  src[:, :, :, 0].rearrange("p g w f -> p (g w) f").unsqueeze(2).broadcast_to([128, 8, 2, HD]),
                                  heads[:, 0, 0:2 * HD].rearrange("p (h f) -> p h f", h=2).unsqueeze(1).broadcast_to([128, 8, 2, HD]),
                                  ALU.mult)
                dve.tensor_tensor(dst[:, :, :, 2], src[:, :, :, 1],
                                  heads[:, :, 2 * HD:].unsqueeze(1).broadcast_to([128, 2, 4, HD]),
                                  ALU.mult).then_inc(v_ready, 1)

            def norm_stats(which, s, src, eps):
                b = ln[which]
                for j in range(WS):
                    last = dve.bn_stats(b["stats"][:, j], src[:, j])
                last.then_inc(stats_done[which], 1)
                st = b["stats"]
                wait(dve, stats_done[which], nth(s, 1, 0))
                dve.tensor_tensor(b["sum"][:], st[:, :, 1], st[:, :, 4], ALU.add)
                dve.tensor_tensor(b["diff"][:], st[:, :, 1], st[:, :, 4], ALU.subtract)
                dve.tensor_tensor(b["dev"][:], st[:, :, 2], st[:, :, 5], ALU.add).then_inc(parts_done[which], 1)
                wait(dve, parts_done[which], nth(s, 1, 0))
                dve.tensor_scalar(b["minus_mean"][:], b["sum"][:], -0.5, None, ALU.mult)
                dve.scalar_tensor_tensor(out=b["between"][:], in0=b["diff"][:], scalar=0.25, in1=b["diff"][:],
                                         op0=ALU.mult, op1=ALU.mult)
                dve.tensor_scalar(b["within"][:], b["dev"][:], 1.0 / C, eps, ALU.mult, ALU.add)\
                    .then_inc(halves_done[which], 1)
                wait(dve, halves_done[which], nth(s, 1, 0))
                dve.tensor_tensor(b["var_eps"][:], b["between"][:], b["within"][:], ALU.add)\
                    .then_inc(ln_ready[which], 1)

            def norm_x(t, phase):
                if not has(t + 2):
                    return
                slot = (phase + 2) % UNROLL
                wait(dve, xn_ready, nth(t + 1, 1, 0))
                wait(dve, xn_rest, nth(t + 1, 1, 0))
                wait(dve, x_loaded[slot], 32 * ((t + 2) // UNROLL + 1))
                norm_stats(0, t + 2, x_in[:, slot], LN_EPS)

            def add_x1(t):
                if not has(t - 1):
                    return
                wait(dve, x1n_ready, nth(t - 1, 1, 0))
                wait(dve, x1n_rest, nth(t - 1, 1, 0))
                wait(dve, x1_ready, nth(t - 1, 2, 1))
                for i, (first, n) in enumerate(((0, 4), (4, 3))):
                    wait(dve, y_psum, nth(t - 1, 2, i))
                    js = slice(first, first + n)
                    dve.tensor_tensor(x1[:, js], bank[i][0:PT_, 0:n * C].rearrange("p (j f) -> p j f", j=n),
                                      x1[:, js], ALU.add).then_inc(y_ready, 1)

            def add_x(t, phase):
                if not has(t):
                    return
                wait(dve, yt_psum, nth(t - 1, 2, 1))
                for i, (first, n, b) in enumerate(((0, 4, 5), (4, 3, 7))):
                    wait(dve, proj_psum, nth(t, 2, i))
                    js = slice(first, first + n)
                    dve.tensor_tensor(x1[:, js], bank[b][0:PT_, 0:n * C].rearrange("p (j f) -> p j f", j=n),
                                      x_in[:, phase, js], ALU.add).then_inc(x1_ready, 1)
                wait(dve, x1_ready, nth(t, 2, 1))
                norm_stats(1, t, x1, LN_EPS)

            def step(t, phase):
                for g in range(3):
                    add_bias(t, phase, g)
                for g in range(3):
                    find_max(t, g)
                tap(t, phase, 0)
                tap(t, phase, 1)
                values(t, phase, 0)
                tap(t, phase, 2)
                values(t, phase, 1)
                norm_x(t, phase)
                if isinstance(t, int) and t == -1:
                    build_table()
                tap(t, phase, 3)
                tap(t, phase, 4)
                for g in range(3):
                    add_up(t, g)
                add_x1(t)
                for i in range(5, 9):
                    tap(t, phase, i)
                add_x(t, phase)

            steps(dve, step)

        @block.gpsimd
        def _(pool):
            pool.memset(bias0, 0.0).then_inc(pool_cleared, 1)
            pool.memset(minus_half[:], -0.5)
            pool.memset(table_load[:], 0.0)
            pool.memset(prob[:], 0.0).then_inc(pool_cleared, 1)
            pool.wait_ge(pool_cleared, 2)
            pool.wait_ge(dve_set, 8)
            pool.tensor_tensor(inv_std, var_eps, minus_half[0:C, 0:1], ALU.pow).then_inc(pool_set, 1)

            def shift(t, g):
                if not has(t):
                    return
                first, n = GROUPS[g]
                wait(pool, max_ready, nth(t, 3, g))
                p = prob[:, HEADS * first:HEADS * (first + n), 0:NT]
                m = smax[:, HEADS * first:HEADS * (first + n)].unsqueeze(2).broadcast_to([128, HEADS * n, NT])
                pool.tensor_tensor(p, p, m, ALU.subtract).then_inc(shifted, 1)

            def divide(t, g):
                if not has(t):
                    return
                first, n = GROUPS[g]
                wait(pool, rec_ready, nth(t, 3, g))
                p = prob[:, HEADS * first:HEADS * (first + n), 0:NT]
                r = srec[:, HEADS * first:HEADS * (first + n)].unsqueeze(2).broadcast_to([128, HEADS * n, NT])
                pool.tensor_tensor(p, p, r, ALU.mult).then_inc(p_ready, 1)

            def root(which, s, dst, src, done):
                b = ln[which]
                wait(pool, ln_ready[which], nth(s, 1, 0))
                pool.tensor_tensor(b["rstd"][:], b["var_eps"][:], minus_half[0:PT_], ALU.pow)\
                    .then_inc(rstd_done[which], 1)
                wait(pool, rstd_done[which], nth(s, 1, 0))
                pool.tensor_tensor(b["offset"][:], b["minus_mean"][:], b["rstd"][:], ALU.mult)\
                    .then_inc(scale_ready[which], 1)
                for j in range(ACT_NORM, WS):
                    last = pool.tensor_scalar(dst[:, j], src[:, j], b["minus_mean"][:, j:j + 1],
                                              b["rstd"][:, j:j + 1], ALU.add, ALU.mult)
                last.then_inc(done, 1)

            def step(t, phase):
                if has(t - 1):
                    wait(pool, x1t_psum, nth(t - 2, 2, 1))
                    root(1, t - 1, x1n, x1, x1n_rest)
                shift(t, 0)
                shift(t, 1)
                shift(t, 2)
                if has(t + 2):
                    wait(pool, xt_psum, nth(t + 1, 2, 1))
                    root(0, t + 2, xn, x_in[:, (phase + 2) % UNROLL], xn_rest)
                for g in range(3):
                    divide(t, g)

            steps(pool, step)


_F = "float32"
_BLOCK = "L0_conv_"
_CONV = "L1_conv_"
_INS = ([_BLOCK + n for n in ("qkv_w", "qkv_b", "proj_w", "proj_b", "rel_bias", "ln1_g", "ln1_b", "ln2_g", "ln2_b",
                              "fc1_w", "fc1_b", "fc2_w", "fc2_b")]
        + [_CONV + n for n in ("dw_kernel", "dw_bias", "pw_kernel", "pw_bias", "gamma", "beta", "moving_mean",
                               "moving_var")])


def constants():
    eye = np.eye(128, dtype=_F)
    rolled = np.zeros((PT_, PT_), _F)
    for r in range(WS):
        for w in range(NWIN):
            rolled[r * NWIN + (w + 1) % NWIN, r * NWIN + w] = 1.0
    col, row = np.arange(NT) // WS, np.arange(NT) % WS
    far_col, far_row = col >= WS - SHIFT, row >= WS - SHIFT
    apart_col = far_col[:, None] != far_col[None, :]
    apart_row = far_row[:, None] != far_row[None, :]
    mask = np.zeros((128, 2, 2, NT), _F)
    for last_strip in range(2):
        for last_pair in range(2):
            for side in range(2):
                apart = (apart_row if last_strip else np.zeros_like(apart_row)) | (
                    apart_col if last_pair and side else np.zeros_like(apart_col))
                mask[64 * side:64 * side + NT, last_strip, last_pair] = np.where(apart, MASKED, 0.0)
    blocks = np.zeros((128, 4, C), _F)
    first, second = slice(0, NT), slice(64, 64 + NT)
    blocks[first, :, 0:HD] = 1.0
    blocks[second, :, HD:2 * HD] = 1.0
    blocks[first, 0:2, 2 * HD:] = 1.0
    blocks[second, 2:4, 2 * HD:] = 1.0
    return {"eye": eye, "rolled_eye": rolled, "mask": mask, "head_blocks": blocks}


def kernel(**inputs):
    import concourse.bacc as bacc
    from concourse.bass_utils import run_bass_kernel_spmd

    nc = bacc.Bacc("TRN2", target_bir_lowering=False, num_devices=1)
    arrays, args = {}, []

    def give(name, a):
        a = np.ascontiguousarray(a)
        arrays[name] = a
        args.append(nc.dram_tensor(name, a.shape, mybir.dt.from_np(a.dtype), kind="ExternalInput").ap())

    give("in_x", inputs["x"])
    for name in _INS:
        a = np.asarray(inputs[name])
        if name.endswith("rel_bias"):
            side = 2 * WS - 1
            a = a.reshape(side, side, HEADS)[::-1, ::-1].transpose(2, 1, 0)
        elif name.endswith("qkv_b"):
            a = a.reshape(3, C).T
        elif name.endswith("fc1_b"):
            a = a.reshape(MC, 128).T
        elif name.endswith("dw_kernel"):
            a = a.reshape(9, C).T
        give("in_" + name, a)
    for name, a in constants().items():
        give("const_" + name, a)
    shape = tuple(inputs["x"].shape)
    args.append(nc.dram_tensor("out_0", shape, F32, kind="ExternalOutput").ap())
    swin_conv_kernel(nc, *args)
    r = run_bass_kernel_spmd(nc, [arrays], core_ids=[0])
    return r.results[0]["out_0"]
```
